# Optimizing a Trainium2 kernel written in Bass

```python
import numpy as np
import jax
import jax.numpy as jnp

def _softmax(x, axis=-1):
    return jax.nn.softmax(x, axis=axis)

def _gelu(x):
    return jax.nn.gelu(x, approximate=True)

def _silu(x):
    return jax.nn.silu(x)

def _sigmoid(x):
    return jax.nn.sigmoid(x)

def _layernorm(x, axis=-1, eps=1e-05):
    m = jnp.mean(x, axis=axis, keepdims=True)
    v = jnp.var(x, axis=axis, keepdims=True)
    return (x - m) / jnp.sqrt(v + eps)

def _scatter_add(tgt, idx, src, axis=0):
    return tgt.at[idx].add(src)

def _segment_sum(src, seg, n):
    return jax.ops.segment_sum(src, seg, n)
kernel_name = 'mk_hybrid_d4_jaxref_r8_be2e78'

def setup_inputs(seed: int=0):
    np.random.seed(seed)
    _w = jnp.asarray

    def _L0_attn_a_setup():
        import jax, jax.numpy as jnp
        from jax import lax
        import numpy as np
        B, L, D_MODEL = (2, 128, 128)
        ED, N, DT_RANK, D_CONV = (256, 16, 64, 4)
        key = jax.random.key(seed)
        ks = jax.random.split(key, 8)
        dt = jnp.exp(jax.random.uniform(ks[6], (ED,)) * (np.log(0.1) - np.log(0.001)) + np.log(0.001))
        dt = jnp.clip(dt, 0.0001, None)
        inv_dt = dt + jnp.log(-jnp.expm1(-dt))
        return {'x': jax.random.normal(ks[0], (B, L, D_MODEL), dtype=jnp.float32), 'in_proj_w': jax.random.normal(ks[1], (D_MODEL, 2 * ED), dtype=jnp.float32) * 0.02, 'conv_w': jax.random.normal(ks[2], (ED, 1, D_CONV), dtype=jnp.float32) * 0.3, 'conv_b': jax.random.normal(ks[3], (ED,), dtype=jnp.float32) * 0.05, 'x_proj_w': jax.random.normal(ks[4], (ED, DT_RANK + 2 * N), dtype=jnp.float32) * 0.02, 'dt_proj_w': jax.random.uniform(ks[5], (DT_RANK, ED), dtype=jnp.float32, minval=-DT_RANK ** (-0.5), maxval=DT_RANK ** (-0.5)), 'dt_proj_b': inv_dt, 'A_log': jnp.log(jnp.tile(jnp.arange(1.0, N + 1.0, dtype=jnp.float32)[None, :], (ED, 1))), 'D': jnp.ones((ED,), dtype=jnp.float32), 'out_proj_w': jax.random.normal(ks[7], (ED, D_MODEL), dtype=jnp.float32) * 0.02}
    _L0_attn_a_in = _L0_attn_a_setup()

    def _L0_attn_b_setup():
        import jax, jax.numpy as jnp
        import numpy as np
        H = 16
        LN_EPS = 1e-05

        def _layernorm(x, g, b):
            mu = jnp.mean(x, axis=-1, keepdims=True)
            var = jnp.mean(jnp.square(x - mu), axis=-1, keepdims=True)
            return (x - mu) * jax.lax.rsqrt(var + LN_EPS) * g + b
        key = jax.random.key(seed)
        ks = jax.random.split(key, 4)
        B, T, D = (32, 128, 128)
        s = 1.0 / np.sqrt(D)
        return {'x': jax.random.normal(ks[0], (B, T, D), dtype=jnp.float32), 'ln_g': jnp.ones((D,), jnp.float32), 'ln_b': jnp.zeros((D,), jnp.float32), 'Wq': jax.random.normal(ks[1], (D, D), dtype=jnp.float32) * s, 'bq': jnp.zeros((D,), jnp.float32), 'Wk': jax.random.normal(ks[2], (D, D), dtype=jnp.float32) * s, 'bk': jnp.zeros((D,), jnp.float32), 'Wv': jax.random.normal(ks[3], (D, D), dtype=jnp.float32) * s, 'bv': jnp.zeros((D,), jnp.float32)}
    _L0_attn_b_in = _L0_attn_b_setup()

    def _L0_ffn_setup():
        import jax, jax.numpy as jnp
        import numpy as np
        B, S, H, F, E, K = (2, 256, 128, 512, 8, 2)

        def _init_w(key, shape, fan_in):
            return jax.random.normal(key, shape, jnp.float32) * fan_in ** (-0.5)

        def _ffn(x, wi, bi, wo, bo):
            return jax.nn.selu(x @ wi + bi) @ wo + bo
        key = jax.random.key(seed)
        ks = jax.random.split(key, 6)
        return {'x': jax.random.normal(ks[0], (B, S, H), jnp.float32), 'gate_wi': _init_w(ks[1], (H, F), H), 'gate_bi': jnp.zeros((F,), jnp.float32), 'gate_wo': _init_w(ks[2], (F, H), F), 'gate_bo': jnp.zeros((H,), jnp.float32), 'exp_wi': _init_w(ks[3], (E, H, F), H), 'exp_bi': jnp.zeros((E, F), jnp.float32), 'exp_wo': _init_w(ks[4], (E, F, H), F), 'exp_bo': jnp.zeros((E, H), jnp.float32)}
    _L0_ffn_in = _L0_ffn_setup()

    def _L1_attn_a_setup():
        import jax, jax.numpy as jnp
        import numpy as np
        D_MODEL = 128
        NUM_HEADS = 16
        D_HEAD = 64
        C = NUM_HEADS * D_HEAD
        WINDOW = 64
        KSIZE = 4
        SCALE = D_HEAD ** (-0.5)

        def _dwconv(x, w, b):
            lhs = x.transpose(0, 2, 1)
            rhs = w[:, None, :]
            y = jax.lax.conv_general_dilated(lhs, rhs, window_strides=(1,), padding=[(KSIZE - 1, 0)], dimension_numbers=('NCH', 'OIH', 'NCH'), feature_group_count=C)
            return (y + b[None, :, None]).transpose(0, 2, 1)

        def _rotary(q, k, seq_len):
            inv_freq = 1.0 / 10000.0 ** (jnp.arange(0, D_HEAD, 2, dtype=jnp.float32) / D_HEAD)
            t = jnp.arange(seq_len, dtype=jnp.float32)
            freqs = t[:, None] * inv_freq[None, :]
            emb = jnp.concatenate([freqs, freqs], axis=-1)
            cos, sin = (jnp.cos(emb), jnp.sin(emb))

            def rot(x):
                x1, x2 = (x[..., :D_HEAD // 2], x[..., D_HEAD // 2:])
                return x * cos + jnp.concatenate([-x2, x1], axis=-1) * sin
            return (rot(q), rot(k))

        def _l2norm(x, eps=1e-12):
            return x / jnp.sqrt(jnp.sum(x * x, axis=-1, keepdims=True) + eps)
        key = jax.random.key(seed)
        ks = jax.random.split(key, 16)
        s = 0.02
        inp = {'x': jax.random.normal(ks[0], (2, 256, D_MODEL), jnp.float32), 'Wq': jax.random.normal(ks[1], (C, D_MODEL), jnp.float32) * s, 'bq': jnp.zeros((C,), jnp.float32), 'Wk': jax.random.normal(ks[2], (C, D_MODEL), jnp.float32) * s, 'bk': jnp.zeros((C,), jnp.float32), 'Wv': jax.random.normal(ks[3], (C, D_MODEL), jnp.float32) * s, 'bv': jnp.zeros((C,), jnp.float32), 'cqw': jax.random.normal(ks[4], (C, KSIZE), jnp.float32) * s, 'cqb': jnp.zeros((C,), jnp.float32), 'ckw': jax.random.normal(ks[5], (C, KSIZE), jnp.float32) * s, 'ckb': jnp.zeros((C,), jnp.float32), 'cvw': jax.random.normal(ks[6], (C, KSIZE), jnp.float32) * s, 'cvb': jnp.zeros((C,), jnp.float32), 'Wo': jax.random.normal(ks[7], (D_MODEL, C), jnp.float32) * s, 'bo': jnp.zeros((D_MODEL,), jnp.float32)}
        return inp
    _L1_attn_a_in = _L1_attn_a_setup()

    def _L1_attn_b_setup():
        import jax, jax.numpy as jnp
        import numpy as np
        import math
        B, L, D = (2, 512, 128)
        H, DK, DV = (4, 32, 32)
        CHUNK = 32
        PROB_FLOOR = 0.02

        def _l2norm(x, eps=1e-06):
            return x * jax.lax.rsqrt(jnp.sum(x * x, -1, keepdims=True) + eps)

        def _silu(x):
            return x * jax.nn.sigmoid(x)

        def _short_conv(x, w):
            K = w.shape[-1]
            xp = jnp.pad(x, ((0, 0), (K - 1, 0), (0, 0)))
            y = sum((xp[:, j:j + x.shape[1], :] * w[:, j] for j in range(K)))
            return _silu(y)

        def _fir_conv(x, filt):
            b, l, h, d = x.shape
            K = filt.shape[-1]
            xf = jnp.pad(x.reshape(b, l, h * d).transpose(0, 2, 1), ((0, 0), (0, 0), (K - 1, 0)))
            w = filt.reshape(h * d, 1, K)
            y = jax.lax.conv_general_dilated(xf, w, (1,), 'VALID', dimension_numbers=('NCH', 'OIH', 'NCH'), feature_group_count=h * d)
            return y.transpose(0, 2, 1).reshape(b, l, h, d)

        def _delta_rule_chunkwise(q, k, v, beta, chunk=CHUNK):
            b, h, Lq, dk = q.shape
            dv = v.shape[-1]
            n = Lq // chunk
            q = _l2norm(q)
            k = _l2norm(k)
            v = v * beta[..., None]
            kb = k * beta[..., None]
            rs = lambda t: t.reshape(b, h, n, chunk, t.shape[-1])
            qc, kc, vc, kbc = (rs(q), rs(k), rs(v), rs(kb))
            strict_lower = jnp.tril(jnp.ones((chunk, chunk), bool), -1)
            M = jnp.where(strict_lower, jnp.einsum('bhncd,bhnmd->bhncm', kbc, kc), 0.0)
            eye = jnp.eye(chunk, dtype=q.dtype)
            T = jax.scipy.linalg.solve_triangular(eye + M, jnp.broadcast_to(eye, M.shape), lower=True, unit_diagonal=True)
            u = T @ vc
            w = T @ kbc
            incl_lower = jnp.tril(jnp.ones((chunk, chunk), bool), 0)

            def step(S, xs):
                q_i, k_i, u_i, w_i = xs
                attn = jnp.where(incl_lower, q_i @ k_i.swapaxes(-1, -2), 0.0)
                u_adj = u_i - w_i @ S
                out_i = q_i @ S + attn @ u_adj
                S = S + k_i.swapaxes(-1, -2) @ u_adj
                return (S, out_i)
            S0 = jnp.zeros((b, h, dk, dv), q.dtype)
            xs = tuple((jnp.moveaxis(t, 2, 0) for t in (qc, kc, u, w)))
            S, out = jax.lax.scan(step, S0, xs)
            out = jnp.moveaxis(out, 0, 2).reshape(b, h, Lq, dv)
            return (out, S)

        def _rmsnorm(x, w, eps=1e-05):
            return x * jax.lax.rsqrt(jnp.mean(x * x, -1, keepdims=True) + eps) * w

        def _per_head_stats(x):
            mean = jnp.mean(x, -1, keepdims=True)
            var = jnp.var(x, -1, keepdims=True)
            am = jnp.mean(jnp.abs(x), -1, keepdims=True)
            l2 = jnp.sqrt(jnp.sum(x * x, -1, keepdims=True))
            return jnp.concatenate([mean, var, am, l2], -1)

        def _forward(hidden_states, q_w, k_w, v_w, b_w, q_cw, k_cw, v_cw, fir_short_w, fir_long_w, mlp1_w, mlp1_b, mlp2_w, mlp2_b, logit_temp, conv_res_logit, norm_w, o_w):
            b, l, _ = hidden_states.shape
            q_in = _short_conv(hidden_states @ q_w.T, q_cw)
            k_in = _short_conv(hidden_states @ k_w.T, k_cw)
            v_in = _short_conv(hidden_states @ v_w.T, v_cw)
            q = q_in.reshape(b, l, H, DK)
            k = k_in.reshape(b, l, H, DK)
            v_direct = v_in.reshape(b, l, H, DV)
            beta = jnp.maximum(jax.nn.sigmoid(hidden_states @ b_w.T), 1e-06)
            delta_out, _S = _delta_rule_chunkwise(q.transpose(0, 2, 1, 3), k.transpose(0, 2, 1, 3), v_direct.transpose(0, 2, 1, 3), beta.transpose(0, 2, 1))
            delta_out = delta_out.transpose(0, 2, 1, 3)
            local_short = _fir_conv(v_direct, fir_short_w)
            local_long = _fir_conv(v_direct, fir_long_w)
            stats = jnp.concatenate([_per_head_stats(local_short), _per_head_stats(local_long), _per_head_stats(delta_out), _per_head_stats(v_direct)], -1)
            hs_exp = jnp.broadcast_to(hidden_states[:, :, None, :], (b, l, H, hidden_states.shape[-1]))
            gate_in = jnp.concatenate([hs_exp, stats], -1)
            h1 = jax.nn.gelu(gate_in @ mlp1_w.T + mlp1_b)
            logits = h1 @ mlp2_w.T + mlp2_b
            temp = jax.nn.softplus(logit_temp)
            p = jax.nn.softmax(logits / temp, -1)
            p = jnp.maximum(p, PROB_FLOOR)
            p = p / jnp.sum(p, -1, keepdims=True)
            o = p[..., 0:1] * local_short + p[..., 1:2] * local_long + p[..., 2:3] * delta_out + p[..., 3:4] * v_direct
            o = o + jax.nn.sigmoid(conv_res_logit)[None, None, :, None] * local_short
            o = _rmsnorm(o, norm_w)
            o = o.reshape(b, l, H * DV) @ o_w.T
            return o
        key = jax.random.key(seed)
        ks = jax.random.split(key, 16)
        s = 0.02
        hidden_gate = D * 2 // 2
        gate_in_dim = D + 16
        inp = {'hidden_states': jax.random.normal(ks[0], (B, L, D), jnp.float32), 'q_w': jax.random.normal(ks[1], (D, D), jnp.float32) * s, 'k_w': jax.random.normal(ks[2], (D, D), jnp.float32) * s, 'v_w': jax.random.normal(ks[3], (D, D), jnp.float32) * s, 'b_w': jax.random.normal(ks[4], (H, D), jnp.float32) * s, 'q_cw': jax.random.normal(ks[5], (D, 4), jnp.float32) * s, 'k_cw': jax.random.normal(ks[6], (D, 4), jnp.float32) * s, 'v_cw': jax.random.normal(ks[7], (D, 4), jnp.float32) * s, 'fir_short_w': jax.random.normal(ks[8], (H, DV, 5), jnp.float32) * s, 'fir_long_w': jax.random.normal(ks[9], (H, DV, 64), jnp.float32) * s, 'mlp1_w': jax.random.normal(ks[10], (hidden_gate, gate_in_dim), jnp.float32) * s, 'mlp1_b': jnp.zeros((hidden_gate,), jnp.float32), 'mlp2_w': jax.random.normal(ks[11], (4, hidden_gate), jnp.float32) * s, 'mlp2_b': jnp.array([-0.5, -0.5, 1.0, 3.0], jnp.float32), 'logit_temp': jnp.full((1,), math.log(math.expm1(0.7)), jnp.float32), 'conv_res_logit': jnp.full((H,), -2.0, jnp.float32), 'norm_w': jnp.ones((DV,), jnp.float32), 'o_w': jax.random.normal(ks[12], (D, D), jnp.float32) * s}
        return inp
    _L1_attn_b_in = _L1_attn_b_setup()

    def _L1_ffn_setup():
        import jax, jax.numpy as jnp
        import numpy as np
        DIM = 128

        def _reference_tuple_inner(x, W_r, W_k, W_v, mu_r, mu_k):
            B, T, C = x.shape
            x_prev = jnp.concatenate([jnp.zeros((B, 1, C), x.dtype), x[:, :-1, :]], axis=1)
            xr = mu_r * x + (1.0 - mu_r) * x_prev
            xk = mu_k * x + (1.0 - mu_k) * x_prev
            r = jax.nn.sigmoid(jnp.einsum('btc,dc->btd', xr, W_r))
            k = jnp.einsum('btc,dc->btd', xk, W_k)
            k_act = jnp.square(jax.nn.relu(k))
            out = r * jnp.einsum('btc,dc->btd', k_act, W_v)
            new_state = x[:, -1, :]
            return (out, new_state)
        key = jax.random.key(seed)
        ks = jax.random.split(key, 6)
        B, T, C = (8, 256, DIM)
        x = jax.random.normal(ks[0], (B, T, C), dtype=jnp.float32)
        s = 1.0 / np.sqrt(C)
        W_r = jax.random.uniform(ks[1], (C, C), jnp.float32, -s, s)
        W_k = jax.random.uniform(ks[2], (C, C), jnp.float32, -s, s)
        W_v = jax.random.uniform(ks[3], (C, C), jnp.float32, -s, s)
        mu_r = jax.random.uniform(ks[4], (C,), jnp.float32)
        mu_k = jax.random.uniform(ks[5], (C,), jnp.float32)
        return {'x': x, 'W_r': W_r, 'W_k': W_k, 'W_v': W_v, 'mu_r': mu_r, 'mu_k': mu_k}
    _L1_ffn_in = _L1_ffn_setup()

    def _L2_attn_a_setup():
        import jax, jax.numpy as jnp
        import numpy as np
        D_MODEL = 128
        EXPAND = 2
        D_INNER = D_MODEL * EXPAND
        D_STATE = 16
        BATCH = 4
        SEQ = 512
        key = jax.random.key(seed)
        ks = jax.random.split(key, 10)
        w = lambda k, shape, scale=0.02: jax.random.normal(k, shape, jnp.float32) * scale
        return {'x': jax.random.normal(ks[0], (BATCH, SEQ, D_MODEL), jnp.float32), 'w_in': w(ks[1], (D_MODEL, D_INNER)), 'b_in': jnp.zeros((D_INNER,), jnp.float32), 'w_gate': w(ks[2], (D_MODEL, D_INNER)), 'b_gate': jnp.zeros((D_INNER,), jnp.float32), 'A': w(ks[3], (D_INNER, D_STATE, D_STATE), 0.05), 'B_ssm': w(ks[4], (D_INNER, D_STATE), 0.1), 'C_ssm': w(ks[5], (D_INNER, D_STATE), 0.1), 'w_out': w(ks[6], (D_INNER, D_MODEL)), 'b_out': jnp.zeros((D_MODEL,), jnp.float32)}
    _L2_attn_a_in = _L2_attn_a_setup()

    def _L2_attn_b_setup():
        import jax, jax.numpy as jnp
        import numpy as np
        D = 128
        K_LOW1 = D // 4
        K_LOW2 = D // 4

        def mix_precision_matmul(x, w):
            d = x.shape[-1]
            w1 = w[:K_LOW1]
            wh = w[K_LOW1:d - K_LOW2]
            w2 = w[d - K_LOW2:]
            y1 = jnp.matmul(x[..., :K_LOW1].astype(jnp.float16), w1.astype(jnp.float16)).astype(jnp.float32)
            yh = jnp.matmul(x[..., K_LOW1:d - K_LOW2], wh)
            y2 = jnp.matmul(x[..., d - K_LOW2:].astype(jnp.float16), w2.astype(jnp.float16)).astype(jnp.float32)
            return y1 + yh + y2
        key = jax.random.key(seed)
        k1, k2, k3, k4 = jax.random.split(key, 4)
        B, N, d = (8, 256, D)
        x = jax.random.normal(k1, (B, N, d), dtype=jnp.float32)
        weight_qkv = jax.random.normal(k2, (d, 3 * d), dtype=jnp.float32) * d ** (-0.5)
        out_w = jax.random.normal(k3, (d, d), dtype=jnp.float32) * d ** (-0.5)
        out_b = jax.random.normal(k4, (d,), dtype=jnp.float32) * 0.01
        return {'x': x, 'weight_qkv': weight_qkv, 'out_w': out_w, 'out_b': out_b}
    _L2_attn_b_in = _L2_attn_b_setup()

    def _L2_ffn_setup():
        import jax, jax.numpy as jnp
        import numpy as np
        ALPHA = 1.0
        key = jax.random.key(seed)
        ks = jax.random.split(key, 7)
        B, S, IN, OUT = (8, 1024, 128, 128)
        RANK, DDIM, UDIM = (4, 100, 50)
        return {'hidden_states': jax.random.normal(ks[0], (B, S, IN), dtype=jnp.float32), 'W': jax.random.normal(ks[1], (OUT, IN), dtype=jnp.float32) * 0.02, 'b': jax.random.normal(ks[2], (OUT,), dtype=jnp.float32) * 0.02, 'lora_down': jax.random.normal(ks[3], (RANK, DDIM), dtype=jnp.float32) * 0.1, 'lora_up': jax.random.normal(ks[4], (UDIM, RANK), dtype=jnp.float32) * 0.1, 'down_aux': jax.random.normal(ks[5], (DDIM, IN), dtype=jnp.float32) * 0.03, 'up_aux': jax.random.normal(ks[6], (OUT, UDIM), dtype=jnp.float32) * 0.03}
    _L2_ffn_in = _L2_ffn_setup()

    def _L3_attn_a_setup():
        import jax, jax.numpy as jnp
        import numpy as np
        B, T, D = (4, 256, 128)
        N_HEADS = 16
        HEAD_DIM = D // N_HEADS

        def rope(x):
            t, dh = (x.shape[-2], x.shape[-1])
            half = dh // 2
            theta = 1.0 / 10000.0 ** (jnp.arange(half, dtype=jnp.float32) / half)
            ang = jnp.arange(t, dtype=jnp.float32)[:, None] * theta[None, :]
            sin, cos = (jnp.sin(ang), jnp.cos(ang))
            x1 = x[..., 0::2]
            x2 = x[..., 1::2]
            return jnp.concatenate([x1 * cos - x2 * sin, x1 * sin + x2 * cos], axis=-1)
        key = jax.random.key(seed)
        ks = jax.random.split(key, 9)
        s = 0.02
        return {'x': jax.random.normal(ks[0], (B, T, D), dtype=jnp.float32), 'W_q': jax.random.normal(ks[1], (D, D), dtype=jnp.float32) * s, 'b_q': jnp.zeros((D,), dtype=jnp.float32), 'W_k': jax.random.normal(ks[2], (D, D), dtype=jnp.float32) * s, 'b_k': jnp.zeros((D,), dtype=jnp.float32), 'W_v': jax.random.normal(ks[3], (D, D), dtype=jnp.float32) * s, 'b_v': jnp.zeros((D,), dtype=jnp.float32), 'W_o': jax.random.normal(ks[4], (D, D), dtype=jnp.float32) * s, 'b_o': jnp.zeros((D,), dtype=jnp.float32)}
    _L3_attn_a_in = _L3_attn_a_setup()

    def _L3_attn_b_setup():
        import jax, jax.numpy as jnp
        import numpy as np
        import math
        D_MODEL = 128
        NUM_HEADS = 16
        HEAD_DIM = D_MODEL // NUM_HEADS
        key = jax.random.key(seed)
        k_x, k_qkv, k_o = jax.random.split(key, 3)
        B, S = (2, 256)
        x = jax.random.normal(k_x, (B, S, D_MODEL), dtype=jnp.float32)
        sigma_qkv = math.sqrt(2.0 / (D_MODEL + 3 * D_MODEL))
        w_qkv = jax.random.truncated_normal(k_qkv, -3.0, 3.0, (3 * D_MODEL, D_MODEL), dtype=jnp.float32) * sigma_qkv
        sigma_o = math.sqrt(2.0 / (D_MODEL + D_MODEL))
        w_out = jax.random.truncated_normal(k_o, -3.0, 3.0, (D_MODEL, D_MODEL), dtype=jnp.float32) * sigma_o
        return {'x': x, 'w_qkv': w_qkv, 'w_out': w_out}
    _L3_attn_b_in = _L3_attn_b_setup()

    def _L3_ffn_setup():
        import jax, jax.numpy as jnp
        import numpy as np
        D_IN, D_HID = (128, 512)

        def _ternary(key, shape):
            return jax.random.randint(key, shape, -1, 2).astype(jnp.float32)

        def _tlin(x, w, s):
            return jnp.einsum('bsi,oi->bso', x, w) * s
        key = jax.random.key(seed)
        ks = jax.random.split(key, 12)
        inv = lambda fan: 1.0 / np.sqrt(fan).astype(np.float32)
        return {'x': jax.random.normal(ks[0], (4, 256, D_IN), dtype=jnp.float32), 'w1_w': _ternary(ks[1], (D_HID, D_IN)), 'w1_s': jax.random.uniform(ks[2], (D_HID,), dtype=jnp.float32) * inv(D_IN), 'w2_w': _ternary(ks[3], (D_HID, D_IN)), 'w2_s': jax.random.uniform(ks[4], (D_HID,), dtype=jnp.float32) * inv(D_IN), 'h1_w': _ternary(ks[5], (D_HID, D_HID)), 'h1_s': jax.random.uniform(ks[6], (D_HID,), dtype=jnp.float32) * inv(D_HID), 'h2_w': _ternary(ks[7], (D_HID, D_HID)), 'h2_s': jax.random.uniform(ks[8], (D_HID,), dtype=jnp.float32) * inv(D_HID), 'w3_w': _ternary(ks[9], (D_IN, D_HID)), 'w3_s': jax.random.uniform(ks[10], (D_IN,), dtype=jnp.float32) * inv(D_HID)}
    _L3_ffn_in = _L3_ffn_setup()
    _d = {'L0_attn_a_x': _L0_attn_a_in['x'], 'L0_attn_a_in_proj_w': _L0_attn_a_in['in_proj_w'], 'L0_attn_a_conv_w': _L0_attn_a_in['conv_w'], 'L0_attn_a_conv_b': _L0_attn_a_in['conv_b'], 'L0_attn_a_x_proj_w': _L0_attn_a_in['x_proj_w'], 'L0_attn_a_dt_proj_w': _L0_attn_a_in['dt_proj_w'], 'L0_attn_a_dt_proj_b': _L0_attn_a_in['dt_proj_b'], 'L0_attn_a_A_log': _L0_attn_a_in['A_log'], 'L0_attn_a_D': _L0_attn_a_in['D'], 'L0_attn_a_out_proj_w': _L0_attn_a_in['out_proj_w'], 'L0_attn_b_ln_g': _L0_attn_b_in['ln_g'], 'L0_attn_b_ln_b': _L0_attn_b_in['ln_b'], 'L0_attn_b_Wq': _L0_attn_b_in['Wq'], 'L0_attn_b_bq': _L0_attn_b_in['bq'], 'L0_attn_b_Wk': _L0_attn_b_in['Wk'], 'L0_attn_b_bk': _L0_attn_b_in['bk'], 'L0_attn_b_Wv': _L0_attn_b_in['Wv'], 'L0_attn_b_bv': _L0_attn_b_in['bv'], 'L0_ffn_gate_wi': _L0_ffn_in['gate_wi'], 'L0_ffn_gate_bi': _L0_ffn_in['gate_bi'], 'L0_ffn_gate_wo': _L0_ffn_in['gate_wo'], 'L0_ffn_gate_bo': _L0_ffn_in['gate_bo'], 'L0_ffn_exp_wi': _L0_ffn_in['exp_wi'], 'L0_ffn_exp_bi': _L0_ffn_in['exp_bi'], 'L0_ffn_exp_wo': _L0_ffn_in['exp_wo'], 'L0_ffn_exp_bo': _L0_ffn_in['exp_bo'], 'L1_attn_a_Wq': _L1_attn_a_in['Wq'], 'L1_attn_a_bq': _L1_attn_a_in['bq'], 'L1_attn_a_Wk': _L1_attn_a_in['Wk'], 'L1_attn_a_bk': _L1_attn_a_in['bk'], 'L1_attn_a_Wv': _L1_attn_a_in['Wv'], 'L1_attn_a_bv': _L1_attn_a_in['bv'], 'L1_attn_a_cqw': _L1_attn_a_in['cqw'], 'L1_attn_a_cqb': _L1_attn_a_in['cqb'], 'L1_attn_a_ckw': _L1_attn_a_in['ckw'], 'L1_attn_a_ckb': _L1_attn_a_in['ckb'], 'L1_attn_a_cvw': _L1_attn_a_in['cvw'], 'L1_attn_a_cvb': _L1_attn_a_in['cvb'], 'L1_attn_a_Wo': _L1_attn_a_in['Wo'], 'L1_attn_a_bo': _L1_attn_a_in['bo'], 'L1_attn_b_q_w': _L1_attn_b_in['q_w'], 'L1_attn_b_k_w': _L1_attn_b_in['k_w'], 'L1_attn_b_v_w': _L1_attn_b_in['v_w'], 'L1_attn_b_b_w': _L1_attn_b_in['b_w'], 'L1_attn_b_q_cw': _L1_attn_b_in['q_cw'], 'L1_attn_b_k_cw': _L1_attn_b_in['k_cw'], 'L1_attn_b_v_cw': _L1_attn_b_in['v_cw'], 'L1_attn_b_fir_short_w': _L1_attn_b_in['fir_short_w'], 'L1_attn_b_fir_long_w': _L1_attn_b_in['fir_long_w'], 'L1_attn_b_mlp1_w': _L1_attn_b_in['mlp1_w'], 'L1_attn_b_mlp1_b': _L1_attn_b_in['mlp1_b'], 'L1_attn_b_mlp2_w': _L1_attn_b_in['mlp2_w'], 'L1_attn_b_mlp2_b': _L1_attn_b_in['mlp2_b'], 'L1_attn_b_logit_temp': _L1_attn_b_in['logit_temp'], 'L1_attn_b_conv_res_logit': _L1_attn_b_in['conv_res_logit'], 'L1_attn_b_norm_w': _L1_attn_b_in['norm_w'], 'L1_attn_b_o_w': _L1_attn_b_in['o_w'], 'L1_ffn_W_r': _L1_ffn_in['W_r'], 'L1_ffn_W_k': _L1_ffn_in['W_k'], 'L1_ffn_W_v': _L1_ffn_in['W_v'], 'L1_ffn_mu_r': _L1_ffn_in['mu_r'], 'L1_ffn_mu_k': _L1_ffn_in['mu_k'], 'L2_attn_a_w_in': _L2_attn_a_in['w_in'], 'L2_attn_a_b_in': _L2_attn_a_in['b_in'], 'L2_attn_a_w_gate': _L2_attn_a_in['w_gate'], 'L2_attn_a_b_gate': _L2_attn_a_in['b_gate'], 'L2_attn_a_A': _L2_attn_a_in['A'], 'L2_attn_a_B_ssm': _L2_attn_a_in['B_ssm'], 'L2_attn_a_C_ssm': _L2_attn_a_in['C_ssm'], 'L2_attn_a_w_out': _L2_attn_a_in['w_out'], 'L2_attn_a_b_out': _L2_attn_a_in['b_out'], 'L2_attn_b_weight_qkv': _L2_attn_b_in['weight_qkv'], 'L2_attn_b_out_w': _L2_attn_b_in['out_w'], 'L2_attn_b_out_b': _L2_attn_b_in['out_b'], 'L2_ffn_W': _L2_ffn_in['W'], 'L2_ffn_b': _L2_ffn_in['b'], 'L2_ffn_lora_down': _L2_ffn_in['lora_down'], 'L2_ffn_lora_up': _L2_ffn_in['lora_up'], 'L2_ffn_down_aux': _L2_ffn_in['down_aux'], 'L2_ffn_up_aux': _L2_ffn_in['up_aux'], 'L3_attn_a_W_q': _L3_attn_a_in['W_q'], 'L3_attn_a_b_q': _L3_attn_a_in['b_q'], 'L3_attn_a_W_k': _L3_attn_a_in['W_k'], 'L3_attn_a_b_k': _L3_attn_a_in['b_k'], 'L3_attn_a_W_v': _L3_attn_a_in['W_v'], 'L3_attn_a_b_v': _L3_attn_a_in['b_v'], 'L3_attn_a_W_o': _L3_attn_a_in['W_o'], 'L3_attn_a_b_o': _L3_attn_a_in['b_o'], 'L3_attn_b_w_qkv': _L3_attn_b_in['w_qkv'], 'L3_attn_b_w_out': _L3_attn_b_in['w_out'], 'L3_ffn_w1_w': _L3_ffn_in['w1_w'], 'L3_ffn_w1_s': _L3_ffn_in['w1_s'], 'L3_ffn_w2_w': _L3_ffn_in['w2_w'], 'L3_ffn_w2_s': _L3_ffn_in['w2_s'], 'L3_ffn_h1_w': _L3_ffn_in['h1_w'], 'L3_ffn_h1_s': _L3_ffn_in['h1_s'], 'L3_ffn_h2_w': _L3_ffn_in['h2_w'], 'L3_ffn_h2_s': _L3_ffn_in['h2_s'], 'L3_ffn_w3_w': _L3_ffn_in['w3_w'], 'L3_ffn_w3_s': _L3_ffn_in['w3_s']}
    _x0 = _d['L0_attn_a_x']
    _d['L0_attn_a_x'] = jax.random.normal(jax.random.fold_in(jax.random.key(seed), 1), (8, 256, 128), dtype=_x0.dtype)
    del _x0
    return _d

def reference(L0_attn_a_x, L0_attn_a_in_proj_w, L0_attn_a_conv_w, L0_attn_a_conv_b, L0_attn_a_x_proj_w, L0_attn_a_dt_proj_w, L0_attn_a_dt_proj_b, L0_attn_a_A_log, L0_attn_a_D, L0_attn_a_out_proj_w, L0_attn_b_ln_g, L0_attn_b_ln_b, L0_attn_b_Wq, L0_attn_b_bq, L0_attn_b_Wk, L0_attn_b_bk, L0_attn_b_Wv, L0_attn_b_bv, L0_ffn_gate_wi, L0_ffn_gate_bi, L0_ffn_gate_wo, L0_ffn_gate_bo, L0_ffn_exp_wi, L0_ffn_exp_bi, L0_ffn_exp_wo, L0_ffn_exp_bo, L1_attn_a_Wq, L1_attn_a_bq, L1_attn_a_Wk, L1_attn_a_bk, L1_attn_a_Wv, L1_attn_a_bv, L1_attn_a_cqw, L1_attn_a_cqb, L1_attn_a_ckw, L1_attn_a_ckb, L1_attn_a_cvw, L1_attn_a_cvb, L1_attn_a_Wo, L1_attn_a_bo, L1_attn_b_q_w, L1_attn_b_k_w, L1_attn_b_v_w, L1_attn_b_b_w, L1_attn_b_q_cw, L1_attn_b_k_cw, L1_attn_b_v_cw, L1_attn_b_fir_short_w, L1_attn_b_fir_long_w, L1_attn_b_mlp1_w, L1_attn_b_mlp1_b, L1_attn_b_mlp2_w, L1_attn_b_mlp2_b, L1_attn_b_logit_temp, L1_attn_b_conv_res_logit, L1_attn_b_norm_w, L1_attn_b_o_w, L1_ffn_W_r, L1_ffn_W_k, L1_ffn_W_v, L1_ffn_mu_r, L1_ffn_mu_k, L2_attn_a_w_in, L2_attn_a_b_in, L2_attn_a_w_gate, L2_attn_a_b_gate, L2_attn_a_A, L2_attn_a_B_ssm, L2_attn_a_C_ssm, L2_attn_a_w_out, L2_attn_a_b_out, L2_attn_b_weight_qkv, L2_attn_b_out_w, L2_attn_b_out_b, L2_ffn_W, L2_ffn_b, L2_ffn_lora_down, L2_ffn_lora_up, L2_ffn_down_aux, L2_ffn_up_aux, L3_attn_a_W_q, L3_attn_a_b_q, L3_attn_a_W_k, L3_attn_a_b_k, L3_attn_a_W_v, L3_attn_a_b_v, L3_attn_a_W_o, L3_attn_a_b_o, L3_attn_b_w_qkv, L3_attn_b_w_out, L3_ffn_w1_w, L3_ffn_w1_s, L3_ffn_w2_w, L3_ffn_w2_s, L3_ffn_h1_w, L3_ffn_h1_s, L3_ffn_h2_w, L3_ffn_h2_s, L3_ffn_w3_w, L3_ffn_w3_s):

    def _L0_attn_a_ref(x, in_proj_w, conv_w, conv_b, x_proj_w, dt_proj_w, dt_proj_b, A_log, D, out_proj_w):
        import jax, jax.numpy as jnp
        from jax import lax
        import numpy as np
        B, L, D_MODEL = (2, 128, 128)
        ED, N, DT_RANK, D_CONV = (256, 16, 64, 4)
        xz = x @ in_proj_w
        xc, z = jnp.split(xz, 2, axis=-1)
        xt = jnp.transpose(xc, (0, 2, 1))
        xt = lax.conv_general_dilated(xt, conv_w, (1,), [(D_CONV - 1, 0)], dimension_numbers=('NCH', 'OIH', 'NCH'), feature_group_count=ED)
        xt = xt + conv_b[None, :, None]
        xc = jax.nn.silu(jnp.transpose(xt, (0, 2, 1)))
        A = -jnp.exp(A_log)
        dbc = xc @ x_proj_w
        delta, Bm, Cm = jnp.split(dbc, [DT_RANK, DT_RANK + N], axis=-1)
        delta = jax.nn.softplus(delta @ dt_proj_w + dt_proj_b)
        deltaA = jnp.exp(delta[..., None] * A)
        BX = delta[..., None] * Bm[:, :, None, :] * xc[..., None]

        def combine(c1, c2):
            a1, x1 = c1
            a2, x2 = c2
            return (a1 * a2, a2 * x1 + x2)
        _, hs = lax.associative_scan(combine, (deltaA, BX), axis=1)
        y = jnp.einsum('blen,bln->ble', hs, Cm) + D * xc
        y = y * jax.nn.silu(z)
        return y @ out_proj_w

    def _L0_attn_b_ref(x, ln_g, ln_b, Wq, bq, Wk, bk, Wv, bv):
        import jax, jax.numpy as jnp
        import numpy as np
        H = 16
        LN_EPS = 1e-05

        def _layernorm(x, g, b):
            mu = jnp.mean(x, axis=-1, keepdims=True)
            var = jnp.mean(jnp.square(x - mu), axis=-1, keepdims=True)
            return (x - mu) * jax.lax.rsqrt(var + LN_EPS) * g + b
        B, T, D = x.shape
        d = D // H
        xn = _layernorm(x, ln_g, ln_b)
        q = jnp.einsum('btd,ed->bte', xn, Wq) + bq
        k = jnp.einsum('btd,ed->bte', xn, Wk) + bk
        v = (jnp.einsum('btd,ed->bte', xn, Wv) + bv).reshape(B, T, H, d)
        q = jax.nn.softmax(q.reshape(B, T, H, d), axis=-1)
        k = jax.nn.softmax(k.reshape(B, T, H, d), axis=1)
        attn = jnp.einsum('bnhd,bnhl->bhdl', k, v)
        y = jnp.einsum('bnhd,bhdl->bnhl', q, attn).reshape(B, T, D)
        return x + y

    def _L0_ffn_ref(x, gate_wi, gate_bi, gate_wo, gate_bo, exp_wi, exp_bi, exp_wo, exp_bo):
        import jax, jax.numpy as jnp
        import numpy as np
        B, S, H, F, E, K = (2, 256, 128, 512, 8, 2)

        def _init_w(key, shape, fan_in):
            return jax.random.normal(key, shape, jnp.float32) * fan_in ** (-0.5)

        def _ffn(x, wi, bi, wo, bo):
            return jax.nn.selu(x @ wi + bi) @ wo + bo
        Bb, Ss, Hh = x.shape
        xf = x.reshape(-1, Hh)
        gate_logits = _ffn(xf, gate_wi, gate_bi, gate_wo, gate_bo)
        topv, topi = jax.lax.top_k(gate_logits, K)
        topv = topv / jnp.sum(topv, axis=-1, keepdims=True)
        onehot = (topi[..., None] == jnp.arange(E)).astype(x.dtype)
        w = jnp.einsum('nk,nke->ne', topv, onehot)
        h = jax.nn.selu(jnp.einsum('nh,ehf->enf', xf, exp_wi) + exp_bi[:, None, :])
        out_e = jnp.einsum('enf,efh->enh', h, exp_wo) + exp_bo[:, None, :]
        out = jnp.einsum('enh,ne->nh', out_e, w)
        return out.reshape(Bb, Ss, Hh)

    def _L1_attn_a_ref(x, Wq, bq, Wk, bk, Wv, bv, cqw, cqb, ckw, ckb, cvw, cvb, Wo, bo):
        import jax, jax.numpy as jnp
        import numpy as np
        D_MODEL = 128
        NUM_HEADS = 16
        D_HEAD = 64
        C = NUM_HEADS * D_HEAD
        WINDOW = 64
        KSIZE = 4
        SCALE = D_HEAD ** (-0.5)

        def _dwconv(x, w, b):
            lhs = x.transpose(0, 2, 1)
            rhs = w[:, None, :]
            y = jax.lax.conv_general_dilated(lhs, rhs, window_strides=(1,), padding=[(KSIZE - 1, 0)], dimension_numbers=('NCH', 'OIH', 'NCH'), feature_group_count=C)
            return (y + b[None, :, None]).transpose(0, 2, 1)

        def _rotary(q, k, seq_len):
            inv_freq = 1.0 / 10000.0 ** (jnp.arange(0, D_HEAD, 2, dtype=jnp.float32) / D_HEAD)
            t = jnp.arange(seq_len, dtype=jnp.float32)
            freqs = t[:, None] * inv_freq[None, :]
            emb = jnp.concatenate([freqs, freqs], axis=-1)
            cos, sin = (jnp.cos(emb), jnp.sin(emb))

            def rot(x):
                x1, x2 = (x[..., :D_HEAD // 2], x[..., D_HEAD // 2:])
                return x * cos + jnp.concatenate([-x2, x1], axis=-1) * sin
            return (rot(q), rot(k))

        def _l2norm(x, eps=1e-12):
            return x / jnp.sqrt(jnp.sum(x * x, axis=-1, keepdims=True) + eps)
        B, S, _ = x.shape
        q = x @ Wq.T + bq
        k = x @ Wk.T + bk
        v = x @ Wv.T + bv
        q = _dwconv(q, cqw, cqb)
        k = _dwconv(k, ckw, ckb)
        v = _dwconv(v, cvw, cvb)
        q = q.reshape(B, S, NUM_HEADS, D_HEAD).transpose(0, 2, 1, 3)
        k = k.reshape(B, S, NUM_HEADS, D_HEAD).transpose(0, 2, 1, 3)
        v = v.reshape(B, S, NUM_HEADS, D_HEAD).transpose(0, 2, 1, 3)
        q, k = _rotary(q, k, S)
        q = _l2norm(q)
        k = _l2norm(k)
        scores = jnp.einsum('bhqd,bhkd->bhqk', q, k) * SCALE
        i = jnp.arange(S)[:, None]
        j = jnp.arange(S)[None, :]
        allowed = (j <= i) & (i - j < WINDOW)
        scores = jnp.where(allowed[None, None], scores, -jnp.inf)
        attn = jax.nn.softmax(scores, axis=-1)
        out = jnp.einsum('bhqk,bhkd->bhqd', attn, v)
        out = out.transpose(0, 2, 1, 3).reshape(B, S, C)
        return out @ Wo.T + bo

    def _L1_attn_b_ref(hidden_states, q_w, k_w, v_w, b_w, q_cw, k_cw, v_cw, fir_short_w, fir_long_w, mlp1_w, mlp1_b, mlp2_w, mlp2_b, logit_temp, conv_res_logit, norm_w, o_w):
        import jax, jax.numpy as jnp
        import numpy as np
        import math
        B, L, D = (2, 512, 128)
        H, DK, DV = (4, 32, 32)
        CHUNK = 32
        PROB_FLOOR = 0.02

        def _l2norm(x, eps=1e-06):
            return x * jax.lax.rsqrt(jnp.sum(x * x, -1, keepdims=True) + eps)

        def _silu(x):
            return x * jax.nn.sigmoid(x)

        def _short_conv(x, w):
            K = w.shape[-1]
            xp = jnp.pad(x, ((0, 0), (K - 1, 0), (0, 0)))
            y = sum((xp[:, j:j + x.shape[1], :] * w[:, j] for j in range(K)))
            return _silu(y)

        def _fir_conv(x, filt):
            b, l, h, d = x.shape
            K = filt.shape[-1]
            xf = jnp.pad(x.reshape(b, l, h * d).transpose(0, 2, 1), ((0, 0), (0, 0), (K - 1, 0)))
            w = filt.reshape(h * d, 1, K)
            y = jax.lax.conv_general_dilated(xf, w, (1,), 'VALID', dimension_numbers=('NCH', 'OIH', 'NCH'), feature_group_count=h * d)
            return y.transpose(0, 2, 1).reshape(b, l, h, d)

        def _delta_rule_chunkwise(q, k, v, beta, chunk=CHUNK):
            b, h, Lq, dk = q.shape
            dv = v.shape[-1]
            n = Lq // chunk
            q = _l2norm(q)
            k = _l2norm(k)
            v = v * beta[..., None]
            kb = k * beta[..., None]
            rs = lambda t: t.reshape(b, h, n, chunk, t.shape[-1])
            qc, kc, vc, kbc = (rs(q), rs(k), rs(v), rs(kb))
            strict_lower = jnp.tril(jnp.ones((chunk, chunk), bool), -1)
            M = jnp.where(strict_lower, jnp.einsum('bhncd,bhnmd->bhncm', kbc, kc), 0.0)
            eye = jnp.eye(chunk, dtype=q.dtype)
            T = jax.scipy.linalg.solve_triangular(eye + M, jnp.broadcast_to(eye, M.shape), lower=True, unit_diagonal=True)
            u = T @ vc
            w = T @ kbc
            incl_lower = jnp.tril(jnp.ones((chunk, chunk), bool), 0)

            def step(S, xs):
                q_i, k_i, u_i, w_i = xs
                attn = jnp.where(incl_lower, q_i @ k_i.swapaxes(-1, -2), 0.0)
                u_adj = u_i - w_i @ S
                out_i = q_i @ S + attn @ u_adj
                S = S + k_i.swapaxes(-1, -2) @ u_adj
                return (S, out_i)
            S0 = jnp.zeros((b, h, dk, dv), q.dtype)
            xs = tuple((jnp.moveaxis(t, 2, 0) for t in (qc, kc, u, w)))
            S, out = jax.lax.scan(step, S0, xs)
            out = jnp.moveaxis(out, 0, 2).reshape(b, h, Lq, dv)
            return (out, S)

        def _rmsnorm(x, w, eps=1e-05):
            return x * jax.lax.rsqrt(jnp.mean(x * x, -1, keepdims=True) + eps) * w

        def _per_head_stats(x):
            mean = jnp.mean(x, -1, keepdims=True)
            var = jnp.var(x, -1, keepdims=True)
            am = jnp.mean(jnp.abs(x), -1, keepdims=True)
            l2 = jnp.sqrt(jnp.sum(x * x, -1, keepdims=True))
            return jnp.concatenate([mean, var, am, l2], -1)

        def _forward(hidden_states, q_w, k_w, v_w, b_w, q_cw, k_cw, v_cw, fir_short_w, fir_long_w, mlp1_w, mlp1_b, mlp2_w, mlp2_b, logit_temp, conv_res_logit, norm_w, o_w):
            b, l, _ = hidden_states.shape
            q_in = _short_conv(hidden_states @ q_w.T, q_cw)
            k_in = _short_conv(hidden_states @ k_w.T, k_cw)
            v_in = _short_conv(hidden_states @ v_w.T, v_cw)
            q = q_in.reshape(b, l, H, DK)
            k = k_in.reshape(b, l, H, DK)
            v_direct = v_in.reshape(b, l, H, DV)
            beta = jnp.maximum(jax.nn.sigmoid(hidden_states @ b_w.T), 1e-06)
            delta_out, _S = _delta_rule_chunkwise(q.transpose(0, 2, 1, 3), k.transpose(0, 2, 1, 3), v_direct.transpose(0, 2, 1, 3), beta.transpose(0, 2, 1))
            delta_out = delta_out.transpose(0, 2, 1, 3)
            local_short = _fir_conv(v_direct, fir_short_w)
            local_long = _fir_conv(v_direct, fir_long_w)
            stats = jnp.concatenate([_per_head_stats(local_short), _per_head_stats(local_long), _per_head_stats(delta_out), _per_head_stats(v_direct)], -1)
            hs_exp = jnp.broadcast_to(hidden_states[:, :, None, :], (b, l, H, hidden_states.shape[-1]))
            gate_in = jnp.concatenate([hs_exp, stats], -1)
            h1 = jax.nn.gelu(gate_in @ mlp1_w.T + mlp1_b)
            logits = h1 @ mlp2_w.T + mlp2_b
            temp = jax.nn.softplus(logit_temp)
            p = jax.nn.softmax(logits / temp, -1)
            p = jnp.maximum(p, PROB_FLOOR)
            p = p / jnp.sum(p, -1, keepdims=True)
            o = p[..., 0:1] * local_short + p[..., 1:2] * local_long + p[..., 2:3] * delta_out + p[..., 3:4] * v_direct
            o = o + jax.nn.sigmoid(conv_res_logit)[None, None, :, None] * local_short
            o = _rmsnorm(o, norm_w)
            o = o.reshape(b, l, H * DV) @ o_w.T
            return o
        return _forward(hidden_states, q_w, k_w, v_w, b_w, q_cw, k_cw, v_cw, fir_short_w, fir_long_w, mlp1_w, mlp1_b, mlp2_w, mlp2_b, logit_temp, conv_res_logit, norm_w, o_w)

    def _L1_ffn_ref(x, W_r, W_k, W_v, mu_r, mu_k):
        import jax, jax.numpy as jnp
        import numpy as np
        DIM = 128

        def _reference_tuple_inner(x, W_r, W_k, W_v, mu_r, mu_k):
            B, T, C = x.shape
            x_prev = jnp.concatenate([jnp.zeros((B, 1, C), x.dtype), x[:, :-1, :]], axis=1)
            xr = mu_r * x + (1.0 - mu_r) * x_prev
            xk = mu_k * x + (1.0 - mu_k) * x_prev
            r = jax.nn.sigmoid(jnp.einsum('btc,dc->btd', xr, W_r))
            k = jnp.einsum('btc,dc->btd', xk, W_k)
            k_act = jnp.square(jax.nn.relu(k))
            out = r * jnp.einsum('btc,dc->btd', k_act, W_v)
            new_state = x[:, -1, :]
            return (out, new_state)
        return _reference_tuple_inner(x, W_r, W_k, W_v, mu_r, mu_k)[0]

    def _L2_attn_a_ref(x, w_in, b_in, w_gate, b_gate, A, B_ssm, C_ssm, w_out, b_out):
        import jax, jax.numpy as jnp
        import numpy as np
        D_MODEL = 128
        EXPAND = 2
        D_INNER = D_MODEL * EXPAND
        D_STATE = 16
        BATCH = 4
        SEQ = 512
        x_proj = x @ w_in + b_in
        gate = jax.nn.sigmoid(x @ w_gate + b_gate)

        def step(h, xt):
            h = jnp.einsum('cnm,bcm->bcn', A, h) + B_ssm[None] * xt[:, :, None]
            y = jnp.einsum('bcn,cn->bc', h, C_ssm)
            return (h, y)
        h0 = jnp.zeros((x.shape[0], D_INNER, D_STATE), x.dtype)
        xs = jnp.swapaxes(x_proj, 0, 1)
        _, ys = jax.lax.scan(step, h0, xs)
        ssm_out = jnp.swapaxes(ys, 0, 1)
        y = ssm_out * gate
        return y @ w_out + b_out

    def _L2_attn_b_ref(x, weight_qkv, out_w, out_b):
        import jax, jax.numpy as jnp
        import numpy as np
        D = 128
        K_LOW1 = D // 4
        K_LOW2 = D // 4

        def mix_precision_matmul(x, w):
            d = x.shape[-1]
            w1 = w[:K_LOW1]
            wh = w[K_LOW1:d - K_LOW2]
            w2 = w[d - K_LOW2:]
            y1 = jnp.matmul(x[..., :K_LOW1].astype(jnp.float16), w1.astype(jnp.float16)).astype(jnp.float32)
            yh = jnp.matmul(x[..., K_LOW1:d - K_LOW2], wh)
            y2 = jnp.matmul(x[..., d - K_LOW2:].astype(jnp.float16), w2.astype(jnp.float16)).astype(jnp.float32)
            return y1 + yh + y2
        d = x.shape[-1]
        qkv = mix_precision_matmul(x, weight_qkv)
        q, k, v = jnp.split(qkv, 3, axis=-1)
        q = q / jnp.sqrt(jnp.asarray(d, dtype=q.dtype))
        qk = jnp.einsum('bqd,bkd->bqk', q, k)
        s = jax.nn.softmax(qk, axis=-1)
        y = jnp.einsum('bqk,bkd->bqd', s, v)
        return jnp.matmul(y, out_w.T) + out_b

    def _L2_ffn_ref(hidden_states, W, b, lora_down, lora_up, down_aux, up_aux):
        import jax, jax.numpy as jnp
        import numpy as np
        ALPHA = 1.0
        lilora_weight = up_aux @ (lora_up @ (lora_down @ down_aux))
        base = jnp.einsum('bsi,oi->bso', hidden_states, W) + b
        delta = jnp.einsum('bsi,oi->bso', hidden_states, lilora_weight)
        return base + ALPHA * delta

    def _L3_attn_a_ref(x, W_q, b_q, W_k, b_k, W_v, b_v, W_o, b_o):
        import jax, jax.numpy as jnp
        import numpy as np
        B, T, D = (4, 256, 128)
        N_HEADS = 16
        HEAD_DIM = D // N_HEADS

        def rope(x):
            t, dh = (x.shape[-2], x.shape[-1])
            half = dh // 2
            theta = 1.0 / 10000.0 ** (jnp.arange(half, dtype=jnp.float32) / half)
            ang = jnp.arange(t, dtype=jnp.float32)[:, None] * theta[None, :]
            sin, cos = (jnp.sin(ang), jnp.cos(ang))
            x1 = x[..., 0::2]
            x2 = x[..., 1::2]
            return jnp.concatenate([x1 * cos - x2 * sin, x1 * sin + x2 * cos], axis=-1)
        b, t, d = x.shape
        h, dh = (N_HEADS, d // N_HEADS)

        def heads(y):
            return y.reshape(b, t, h, dh).transpose(0, 2, 1, 3)
        q = rope(heads(x @ W_q.T + b_q))
        k = rope(heads(x @ W_k.T + b_k))
        v = heads(x @ W_v.T + b_v)
        scores = jnp.einsum('bhtd,bhsd->bhts', q, k)
        causal = jnp.tril(jnp.ones((t, t), dtype=bool))
        mask = jnp.where(causal, 0.0, -jnp.inf)
        probs = jax.nn.softmax((scores + mask) / jnp.sqrt(jnp.float32(dh)), axis=-1)
        out = jnp.einsum('bhts,bhsd->bhtd', probs, v)
        out = out.transpose(0, 2, 1, 3).reshape(b, t, d)
        return out @ W_o.T + b_o

    def _L3_attn_b_ref(x, w_qkv, w_out):
        import jax, jax.numpy as jnp
        import numpy as np
        import math
        D_MODEL = 128
        NUM_HEADS = 16
        HEAD_DIM = D_MODEL // NUM_HEADS
        B, S, _ = x.shape
        qkv = jnp.einsum('bsi,oi->bso', x, w_qkv)
        q, k, v = jnp.split(qkv, 3, axis=-1)

        def to_heads(t):
            return t.reshape(B, S, NUM_HEADS, HEAD_DIM).transpose(0, 2, 1, 3)
        q, k, v = (to_heads(q), to_heads(k), to_heads(v))
        scale = 1.0 / math.sqrt(HEAD_DIM)
        logits = jnp.einsum('bhsd,bhtd->bhst', q, k) * scale
        mask = jnp.tril(jnp.ones((S, S), dtype=bool))
        neg_inf = jnp.finfo(jnp.float32).min
        logits = jnp.where(mask, logits, neg_inf)
        probs = jax.nn.softmax(logits, axis=-1)
        probs = probs * mask.astype(probs.dtype)
        out = jnp.einsum('bhst,bhtd->bhsd', probs, v)
        out = out.transpose(0, 2, 1, 3).reshape(B, S, D_MODEL)
        return jnp.einsum('bsi,oi->bso', out, w_out)

    def _L3_ffn_ref(x, w1_w, w1_s, w2_w, w2_s, h1_w, h1_s, h2_w, h2_s, w3_w, w3_s):
        import jax, jax.numpy as jnp
        import numpy as np
        D_IN, D_HID = (128, 512)

        def _ternary(key, shape):
            return jax.random.randint(key, shape, -1, 2).astype(jnp.float32)

        def _tlin(x, w, s):
            return jnp.einsum('bsi,oi->bso', x, w) * s
        h = jax.nn.silu(_tlin(x, w1_w, w1_s)) * _tlin(x, w2_w, w2_s)
        h = jax.nn.gelu(_tlin(h, h1_w, h1_s), approximate=False)
        h = jax.nn.gelu(_tlin(h, h2_w, h2_s), approximate=False)
        return _tlin(h, w3_w, w3_s)
    x = L0_attn_a_x
    x = x + _L0_attn_a_ref(_layernorm(x, axis=-1), L0_attn_a_in_proj_w, L0_attn_a_conv_w, L0_attn_a_conv_b, L0_attn_a_x_proj_w, L0_attn_a_dt_proj_w, L0_attn_a_dt_proj_b, L0_attn_a_A_log, L0_attn_a_D, L0_attn_a_out_proj_w)
    x = x + _L0_ffn_ref(_layernorm(x, axis=-1), L0_ffn_gate_wi, L0_ffn_gate_bi, L0_ffn_gate_wo, L0_ffn_gate_bo, L0_ffn_exp_wi, L0_ffn_exp_bi, L0_ffn_exp_wo, L0_ffn_exp_bo)
    x = x + _L0_attn_b_ref(_layernorm(x, axis=-1), L0_attn_b_ln_g, L0_attn_b_ln_b, L0_attn_b_Wq, L0_attn_b_bq, L0_attn_b_Wk, L0_attn_b_bk, L0_attn_b_Wv, L0_attn_b_bv)
    x = x + _L0_ffn_ref(_layernorm(x, axis=-1), L0_ffn_gate_wi, L0_ffn_gate_bi, L0_ffn_gate_wo, L0_ffn_gate_bo, L0_ffn_exp_wi, L0_ffn_exp_bi, L0_ffn_exp_wo, L0_ffn_exp_bo)
    x = x + _L1_attn_a_ref(_layernorm(x, axis=-1), L1_attn_a_Wq, L1_attn_a_bq, L1_attn_a_Wk, L1_attn_a_bk, L1_attn_a_Wv, L1_attn_a_bv, L1_attn_a_cqw, L1_attn_a_cqb, L1_attn_a_ckw, L1_attn_a_ckb, L1_attn_a_cvw, L1_attn_a_cvb, L1_attn_a_Wo, L1_attn_a_bo)
    x = x + _L1_ffn_ref(_layernorm(x, axis=-1), L1_ffn_W_r, L1_ffn_W_k, L1_ffn_W_v, L1_ffn_mu_r, L1_ffn_mu_k)
    x = x + _L1_attn_b_ref(_layernorm(x, axis=-1), L1_attn_b_q_w, L1_attn_b_k_w, L1_attn_b_v_w, L1_attn_b_b_w, L1_attn_b_q_cw, L1_attn_b_k_cw, L1_attn_b_v_cw, L1_attn_b_fir_short_w, L1_attn_b_fir_long_w, L1_attn_b_mlp1_w, L1_attn_b_mlp1_b, L1_attn_b_mlp2_w, L1_attn_b_mlp2_b, L1_attn_b_logit_temp, L1_attn_b_conv_res_logit, L1_attn_b_norm_w, L1_attn_b_o_w)
    x = x + _L1_ffn_ref(_layernorm(x, axis=-1), L1_ffn_W_r, L1_ffn_W_k, L1_ffn_W_v, L1_ffn_mu_r, L1_ffn_mu_k)
    x = x + _L2_attn_a_ref(_layernorm(x, axis=-1), L2_attn_a_w_in, L2_attn_a_b_in, L2_attn_a_w_gate, L2_attn_a_b_gate, L2_attn_a_A, L2_attn_a_B_ssm, L2_attn_a_C_ssm, L2_attn_a_w_out, L2_attn_a_b_out)
    x = x + _L2_ffn_ref(_layernorm(x, axis=-1), L2_ffn_W, L2_ffn_b, L2_ffn_lora_down, L2_ffn_lora_up, L2_ffn_down_aux, L2_ffn_up_aux)
    x = x + _L2_attn_b_ref(_layernorm(x, axis=-1), L2_attn_b_weight_qkv, L2_attn_b_out_w, L2_attn_b_out_b)
    x = x + _L2_ffn_ref(_layernorm(x, axis=-1), L2_ffn_W, L2_ffn_b, L2_ffn_lora_down, L2_ffn_lora_up, L2_ffn_down_aux, L2_ffn_up_aux)
    x = x + _L3_attn_a_ref(_layernorm(x, axis=-1), L3_attn_a_W_q, L3_attn_a_b_q, L3_attn_a_W_k, L3_attn_a_b_k, L3_attn_a_W_v, L3_attn_a_b_v, L3_attn_a_W_o, L3_attn_a_b_o)
    x = x + _L3_ffn_ref(_layernorm(x, axis=-1), L3_ffn_w1_w, L3_ffn_w1_s, L3_ffn_w2_w, L3_ffn_w2_s, L3_ffn_h1_w, L3_ffn_h1_s, L3_ffn_h2_w, L3_ffn_h2_s, L3_ffn_w3_w, L3_ffn_w3_s)
    x = x + _L3_attn_b_ref(_layernorm(x, axis=-1), L3_attn_b_w_qkv, L3_attn_b_w_out)
    x = x + _L3_ffn_ref(_layernorm(x, axis=-1), L3_ffn_w1_w, L3_ffn_w1_s, L3_ffn_w2_w, L3_ffn_w2_s, L3_ffn_h1_w, L3_ffn_h1_s, L3_ffn_h2_w, L3_ffn_h2_s, L3_ffn_w3_w, L3_ffn_w3_s)
    return x

_drawn_inputs = setup_inputs


def setup_inputs(seed=0):
    import zlib

    import numpy as np

    out = dict(_drawn_inputs(seed))
    spreads = {'L0_attn_a_D': (1.0, 0.2),
     'L0_attn_b_ln_g': (1.0, 0.2),
     'L0_attn_b_ln_b': (0.0, 0.1),
     'L0_attn_b_bq': (0.0, 0.1),
     'L0_attn_b_bk': (0.0, 0.1),
     'L0_attn_b_bv': (0.0, 0.1),
     'L0_ffn_gate_bi': (0.0, 0.1),
     'L0_ffn_gate_bo': (0.0, 0.1),
     'L0_ffn_exp_bi': (0.0, 0.1),
     'L0_ffn_exp_bo': (0.0, 0.1),
     'L1_attn_a_bq': (0.0, 0.1),
     'L1_attn_a_bk': (0.0, 0.1),
     'L1_attn_a_bv': (0.0, 0.1),
     'L1_attn_a_cqb': (0.0, 0.1),
     'L1_attn_a_ckb': (0.0, 0.1),
     'L1_attn_a_cvb': (0.0, 0.1),
     'L1_attn_a_bo': (0.0, 0.1),
     'L1_attn_b_mlp1_b': (0.0, 0.1),
     'L1_attn_b_conv_res_logit': (-2.0, 0.2),
     'L1_attn_b_norm_w': (1.0, 0.2),
     'L2_attn_a_b_in': (0.0, 0.1),
     'L2_attn_a_b_gate': (0.0, 0.1),
     'L2_attn_a_b_out': (0.0, 0.1),
     'L3_attn_a_b_q': (0.0, 0.1),
     'L3_attn_a_b_k': (0.0, 0.1),
     'L3_attn_a_b_v': (0.0, 0.1),
     'L3_attn_a_b_o': (0.0, 0.1)}
    factors = {}
    for name, (base, spread) in spreads.items():
        noise = np.random.default_rng([zlib.crc32(name.encode()), seed]).standard_normal(out[name].shape)
        drawn = base * np.exp(spread * noise) if base else spread * noise
        out[name] = jnp.asarray(drawn.astype(out[name].dtype))
    for name, factor in factors.items():
        out[name] = (out[name] * factor).astype(out[name].dtype)
    return out
```

```python
from contextlib import ExitStack, contextmanager

import numpy as np
import concourse.bass as bass
from concourse import mybir

F32 = mybir.dt.float32
F16 = mybir.dt.float16
BF16 = mybir.dt.bfloat16
ALU = mybir.AluOpType
ACT = mybir.ActivationFunctionType
X = mybir.AxisListType.X

P = 128
BATCHES = 8
T = 256
SEQS = 2
TOK = SEQS * T
NT = TOK // P
PASSES = BATCHES // SEQS
TPS = T // P


class Named(dict):

    def __getattr__(self, name):
        return self[name]


class Steps:

    def __init__(self, eng):
        self.eng = eng
        self.sent = []

    def count(self, sem):
        return sum(1 for s in self.sent if s is sem)

    def tell(self, ins, sem):
        ins.then_inc(sem, 1)
        self.sent.append(sem)

    def __call__(self, ins, sem):
        self.tell(ins, sem)
        self.eng.wait_ge(sem, self.count(sem))


@contextmanager
def stage(m, names):
    nc = m.nc
    m.stages += 1
    sems = {n: nc.alloc_semaphore(f"{n}_{m.stages}") for n in names.split()}
    with nc.Block() as block:
        yield block, Named(sems)
    for sem in sems.values():
        nc.gpsimd.sem_clear(sem)
    for sem in m.resting:
        nc.release_semaphore(sem)
    m.resting = list(sems.values())


@contextmanager
def buffers(m, **shapes):
    with ExitStack() as ctx:
        out = {}
        for name, shape in shapes.items():
            m.made += 1
            dt = F32
            if isinstance(shape, tuple):
                shape, dt = shape
            out[name] = ctx.enter_context(m.nc.sbuf_tensor(f"{name}_{m.made}", shape, dt))
        yield Named(out)


def loaded(m, eng, *groups):
    for g in groups:
        eng.wait_ge(m.load[g], 16)


def normalize(m, src, tok, dst, gamma=None, beta=None, groups=()):
    with buffers(m, stats=[P, NT, 6], moments=[P, NT, 2], shifted=[P, NT], rstd=[P, NT]) as b, \
            stage(m, "stats moments shifted rstd centred turned copied") as (block, s):
        @block.vector
        def _(ve):
            for t in range(NT):
                ve.bn_stats(b.stats[:, t, :], src[:, t, :]).then_inc(s.stats, 1)
            for t in range(NT):
                ve.wait_ge(s.stats, t + 1)
                ve.bn_aggr(b.moments[:, t, :], b.stats[:, t, :]).then_inc(s.moments, 1)
            ve.wait_ge(s.rstd, 1)
            for t in range(NT):
                ve.tensor_scalar(tok[:, t, :], src[:, t, :], b.moments[:, t, 0:1], b.rstd[:, t:t + 1],
                                 ALU.subtract, ALU.mult).then_inc(s.centred, 1)

        @block.gpsimd
        def _(po):
            po.wait_ge(s.moments, NT)
            po.tensor_scalar(b.shifted[:, :], b.moments[:, :, 1], 1e-5, None, ALU.add).then_inc(s.shifted, 1)
            po.wait_ge(s.shifted, 1)
            po.tensor_tensor(b.rstd[:, :], b.shifted[:, :], m.minus_half[:, 0:NT], ALU.pow).then_inc(s.rstd, 1)

        @block.tensor
        def _(pe):
            for t in range(NT):
                pe.wait_ge(s.centred, t + 1)
                pe.transpose(m.ps[:, t % 4, 0:P], tok[:, t, :], m.ident).then_inc(s.turned, 1)

        @block.scalar
        def _(act):
            if gamma is not None:
                loaded(m, act, *groups)
            for t in range(NT):
                act.wait_ge(s.turned, t + 1)
                if gamma is None:
                    act.activation(dst(t), m.ps[:, t % 4, 0:P], ACT.Copy).then_inc(s.copied, 1)
                else:
                    act.activation(dst(t), m.ps[:, t % 4, 0:P], ACT.Identity, bias=beta,
                                   scale=gamma).then_inc(s.copied, 1)
            act.wait_ge(s.copied, NT)


def flat(xT):
    return lambda t: xT[:, t * P:(t + 1) * P]


def padded(xT, pad):
    return lambda t: xT[:, t // TPS, pad + (t % TPS) * P:pad + (t % TPS + 1) * P]


def tile(a, t):
    return a[:, t * P:(t + 1) * P]



def mamba(m, x, tok, xT):
    w = m.w
    ED_TILES, N = 2, 16
    RANK = 64
    normalize(m, x, tok, flat(xT))
    with buffers(m, conv_in=[P, ED_TILES, SEQS, 3 + T], gate=[P, ED_TILES, TOK], conv=[P, ED_TILES, TOK],
                 xs=[P, ED_TILES, TOK], low=[RANK, TOK],
                 bc_rest=[96, TOK], bc_mid=([96, TOK], BF16), bc=([96, TOK], BF16), pick=([96, 2 * N], BF16),
                 thrice=[P, ED_TILES, 3 * 2 * N], soft=[P, ED_TILES, TOK],
                 delta=[P, ED_TILES, TOK], dx=[P, ED_TILES, TOK], rate=[P, ED_TILES * N],
                 decay=[P, 2, ED_TILES, TOK], drive=[P, ED_TILES, TOK], state=[P, 3, ED_TILES, TOK],
                 c_rows=[P, 2, TOK], part=[P, 2, ED_TILES, TOK], y=[P, ED_TILES, TOK]) as b:
        with stage(m, "projected copied gated cleared convolved active low_made low_copied stepped pick bc "
                      "absolute decayed logged rectified delta rate dx") as (block, s):
            @block.tensor
            def _(pe):
                loaded(m, pe, "l0a")
                for c in range(2 * ED_TILES):
                    pe.matmul(m.ps[:, c, :], tile(w.in_proj, c), xT[:, :], start=True,
                              stop=True).then_inc(s.projected, 1)
                pe.wait_ge(s.pick, 2 + ED_TILES)
                for c in range(ED_TILES):
                    pe.wait_ge(s.active, c + 1)
                    pe.matmul(m.ps[0:RANK, 4, :], w.x_proj[:, c * 96:c * 96 + RANK], b.xs[:, c, :],
                              start=(c == 0), stop=(c == ED_TILES - 1)).then_inc(s.low_made, 1)
                    pe.matmul(m.ps[0:96, 5, :], b.thrice[:, c, :], b.xs[:, c, :],
                              start=(c == 0), stop=(c == ED_TILES - 1)).then_inc(s.low_made, 1)
                pe.wait_ge(s.low_copied, 1)
                for c in range(ED_TILES):
                    pe.matmul(m.ps[:, 6 + c, :], w.dt_proj[0:RANK, c * P:(c + 1) * P], b.low[:, :],
                              start=True, stop=True).then_inc(s.stepped, 1)

            @block.scalar
            def _(act):
                loaded(m, act, "l0a")
                for c in range(ED_TILES):
                    act.wait_ge(s.projected, c + 1)
                    act.activation(b.conv_in[:, c, :, 3:], m.ps[:, c, :].rearrange("p (b t) -> p b t", b=SEQS),
                                   ACT.Copy).then_inc(s.copied, 1)
                for c in range(ED_TILES):
                    act.wait_ge(s.projected, ED_TILES + c + 1)
                    act.activation(b.gate[:, c, :], m.ps[:, ED_TILES + c, :], ACT.Silu).then_inc(s.gated, 1)
                for c in range(ED_TILES):
                    act.wait_ge(s.convolved, 4 * (c + 1))
                    act.activation(b.xs[:, c, :], b.conv[:, c, :], ACT.Silu).then_inc(s.active, 1)
                act.wait_ge(s.low_made, 2 * ED_TILES)
                act.activation(b.low[:, :], m.ps[0:RANK, 4, :], ACT.Copy).then_inc(s.low_copied, 1)
                act.activation(b.bc[:, :], m.ps[0:96, 5, :], ACT.Copy).then_inc(s.low_copied, 1)
                for c in range(ED_TILES):
                    act.wait_ge(s.stepped, c + 1)
                    act.activation(b.soft[:, c, :], m.ps[:, 6 + c, :], ACT.Abs,
                                   bias=w.dt_bias[:, c:c + 1]).then_inc(s.absolute, 1)
                for c in range(ED_TILES):
                    act.wait_ge(s.absolute, c + 1)
                    act.activation(b.soft[:, c, :], b.soft[:, c, :], ACT.Exp, scale=-1.0).then_inc(s.decayed, 1)
                act.activation(b.rate[:, :], w.A_log, ACT.Exp).then_inc(s.decayed, 1)
                for c in range(ED_TILES):
                    act.wait_ge(s.decayed, c + 1)
                    act.activation(b.soft[:, c, :], b.soft[:, c, :], ACT.Ln, bias=1.0).then_inc(s.logged, 1)

            @block.vector
            def _(ve):
                step = Steps(ve)
                loaded(m, ve, "l0a")
                step(ve.memset(b.conv_in[:, :, :, 0:3], 0.0), s.cleared)
                for c in range(ED_TILES):
                    ve.wait_ge(s.copied, c + 1)
                    out = b.conv[:, c, :].rearrange("p (b t) -> p b t", b=SEQS)
                    step(ve.tensor_scalar(out, b.conv_in[:, c, :, 0:T], w.conv_w[:, 4 * c:4 * c + 1],
                                          w.conv_b[:, c:c + 1], ALU.mult, ALU.add), s.convolved)
                    for j in range(1, 4):
                        step(ve.scalar_tensor_tensor(out, b.conv_in[:, c, :, j:j + T],
                                                     w.conv_w[:, 4 * c + j:4 * c + j + 1], out,
                                                     ALU.mult, ALU.add), s.convolved)
                ve.wait_ge(s.low_copied, 2)
                step(ve.tensor_tensor(b.bc_rest[:, :], m.ps[0:96, 5, :], b.bc[:, :], ALU.subtract), s.bc)
                step(ve.tensor_copy(b.bc_mid[:, :], b.bc_rest[:, :]), s.bc)
                step(ve.tensor_copy(b.bc[32:64, :], b.bc_mid[32:64, :]), s.bc)
                step(ve.tensor_tensor(b.bc[64:96, :], b.bc_rest[64:96, :], b.bc_mid[64:96, :], ALU.subtract), s.bc)
                for c in range(ED_TILES):
                    ve.wait_ge(s.stepped, c + 1)
                    ve.wait_ge(s.absolute, c + 1)
                    step(ve.tensor_scalar(b.delta[:, c, :], m.ps[:, 6 + c, :], w.dt_bias[:, c:c + 1], 0.0,
                                          ALU.add, ALU.max), s.rectified)
                    ve.wait_ge(s.logged, c + 1)
                    step(ve.tensor_tensor(b.delta[:, c, :], b.delta[:, c, :], b.soft[:, c, :], ALU.add), s.delta)
                    ve.tensor_tensor(b.dx[:, c, :], b.delta[:, c, :], b.xs[:, c, :], ALU.mult).then_inc(s.dx, 1)
                ve.wait_ge(s.decayed, ED_TILES + 1)
                step(ve.tensor_scalar(b.rate[:, :], b.rate[:, :], -1.0, None, ALU.mult), s.rate)
                ve.wait_ge(s.dx, ED_TILES)

            @block.gpsimd
            def _(po):
                step = Steps(po)
                step(po.tensor_tensor(b.pick[:, :], m.ident16[0:96, 0:32], m.ident16[0:96, 32:64], ALU.add), s.pick)
                step(po.tensor_tensor(b.pick[:, :], b.pick[:, :], m.ident16[0:96, 64:96], ALU.add), s.pick)
                loaded(m, po, "l0a")
                for c in range(ED_TILES):
                    step(po.tensor_copy(b.thrice[:, c, :].rearrange("p (r n) -> p r n", r=3),
                                        w.x_proj[:, c * 96 + RANK:c * 96 + 96].unsqueeze(1)
                                        .to_broadcast([P, 3, 2 * N])), s.pick)

        with stage(m, "b_spread c_spread c_copied decay drive state part added") as (block, s):
            @block.tensor
            def _(pe):
                def add_part(n):
                    for c in range(ED_TILES):
                        pe.wait_ge(s.part, ED_TILES * n + c + 1)
                        pe.matmul(m.ps[:, 4 + c, :], m.ident, b.part[:, n % 2, c, :], start=(n == 0),
                                  stop=(n == N - 1)).then_inc(s.added, 1)

                def spread_b(n):
                    if n >= 2:
                        pe.wait_ge(s.drive, ED_TILES * (n - 1))
                    pe.matmul(m.ps[:, n % 2, :], b.pick[:, n:n + 1].to_broadcast([96, P]), b.bc[:, :],
                              start=True, stop=True).then_inc(s.b_spread, 1)

                spread_b(0)
                for n in range(N):
                    if n >= 2:
                        pe.wait_ge(s.c_copied, n - 1)
                    pe.matmul(m.ps[:, 2 + n % 2, :], b.pick[:, N + n:N + n + 1].to_broadcast([96, P]),
                              b.bc[:, :], start=True, stop=True).then_inc(s.c_spread, 1)
                    if n + 1 < N:
                        spread_b(n + 1)
                    if n >= 2:
                        add_part(n - 2)
                add_part(N - 2)
                add_part(N - 1)

            @block.scalar
            def _(act):
                for n in range(N):
                    for c in range(ED_TILES):
                        if n >= 2:
                            act.wait_ge(s.state, ED_TILES * SEQS * (n - 2) + SEQS * (c + 1))
                        act.activation(b.decay[:, n % 2, c, :], b.delta[:, c, :], ACT.Exp,
                                       scale=b.rate[:, N * c + n:N * c + n + 1]).then_inc(s.decay, 1)
                    act.wait_ge(s.c_spread, n + 1)
                    if n >= 2:
                        act.wait_ge(s.part, ED_TILES * (n - 1))
                    act.activation(b.c_rows[:, n % 2, :], m.ps[:, 2 + n % 2, :], ACT.Copy).then_inc(s.c_copied, 1)

            @block.vector
            def _(ve):
                for n in range(N):
                    ve.wait_ge(s.b_spread, n + 1)
                    for c in range(ED_TILES):
                        if n >= 1:
                            ve.wait_ge(s.state, ED_TILES * SEQS * (n - 1) + SEQS * (c + 1))
                        ve.tensor_tensor(b.drive[:, c, :], b.dx[:, c, :], m.ps[:, n % 2, :],
                                         ALU.mult).then_inc(s.drive, 1)
                    for c in range(ED_TILES):
                        ve.wait_ge(s.drive, ED_TILES * n + c + 1)
                        ve.wait_ge(s.decay, ED_TILES * n + c + 1)
                        if n >= 3:
                            ve.wait_ge(s.part, ED_TILES * (n - 3) + c + 1)
                        for q in range(SEQS):
                            r = slice(q * T, (q + 1) * T)
                            ve.tensor_tensor_scan(b.state[:, n % 3, c, r], b.decay[:, n % 2, c, r],
                                                  b.drive[:, c, r], 0.0, ALU.mult, ALU.add).then_inc(s.state, 1)

            @block.gpsimd
            def _(po):
                for n in range(N):
                    po.wait_ge(s.c_copied, n + 1)
                    for c in range(ED_TILES):
                        po.wait_ge(s.state, ED_TILES * SEQS * n + SEQS * (c + 1))
                        if n >= 2:
                            po.wait_ge(s.added, ED_TILES * (n - 2) + c + 1)
                        po.tensor_tensor(b.part[:, n % 2, c, :], b.state[:, n % 3, c, :], b.c_rows[:, n % 2, :],
                                         ALU.mult).then_inc(s.part, 1)

        with stage(m, "skipped gated projected summed") as (block, s):
            @block.vector
            def _(ve):
                step = Steps(ve)
                for c in range(ED_TILES):
                    step(ve.scalar_tensor_tensor(b.y[:, c, :], b.xs[:, c, :], w.D[:, c:c + 1], m.ps[:, 4 + c, :],
                                                 ALU.mult, ALU.add), s.skipped)
                    step(ve.tensor_tensor(b.y[:, c, :], b.y[:, c, :], b.gate[:, c, :], ALU.mult), s.gated)
                ve.wait_ge(s.projected, NT)
                step(ve.tensor_tensor(x[:, :, :], x[:, :, :], m.tiles(0), ALU.add), s.summed)

            @block.tensor
            def _(pe):
                pe.wait_ge(s.gated, ED_TILES)
                for t in range(NT):
                    for c in range(ED_TILES):
                        mm = pe.matmul(m.tiles(0)[:, t, :], tile(b.y[:, c, :], t), tile(w.out_proj, c),
                                       start=(c == 0), stop=(c == ED_TILES - 1))
                    mm.then_inc(s.projected, 1)



SELU_ALPHA = 1.6732632423543772848170429916717
SELU_SCALE = 1.0507009873554804934193349852946


def experts(m, x, tok, xT):
    w = m.w
    E, FC = 8, 4
    NETS = E + 1
    normalize(m, x, tok, flat(xT))
    with buffers(m, grown=[P, 4, TOK], kept=[P, 4, TOK], hidden=[P, 8, TOK], logits=[P, NT, P],
                 top=[P, NT, 8], both=[P, NT], weight=[P, NT, E], scaled=[P, NT, E], turned=[E, TOK]) as b, \
            stage(m, "up grown kept fell hidden down logits top both share weight scaled combined "
                     "turned turned_copied bias summed") as (block, s):
        @block.tensor
        def _(pe):
            loaded(m, pe, "ffn")

            def up(e):
                for f in range(FC):
                    k = FC * e + f
                    if k >= 4:
                        pe.wait_ge(s.grown, k - 3)
                        pe.wait_ge(s.kept, k - 3)
                    pe.matmul(m.ps[:, k % 4, :], tile(w.ffn_wi, k), xT[:, :], start=True,
                              stop=True).then_inc(s.up, 1)

            def down(e):
                pe.wait_ge(s.hidden, FC * (e + 1))
                if e == 2:
                    pe.wait_ge(s.logits, 1)
                if e >= 3:
                    pe.wait_ge(s.combined, NT * (e - 2))
                for t in range(NT):
                    for f in range(FC):
                        mm = pe.matmul(m.tiles(4 + e % 2)[:, t, :], tile(b.hidden[:, (FC * e + f) % 8, :], t),
                                       tile(w.ffn_wo, FC * e + f), start=(f == 0), stop=(f == FC - 1))
                mm.then_inc(s.down, 1)

            for e in range(NETS):
                up(e)
                if e >= 1:
                    down(e - 1)
            down(NETS - 1)
            pe.wait_ge(s.weight, NT)
            for t in range(NT):
                pe.transpose(m.ps[0:E, 6, tile_of(t)], b.weight[:, t, :], m.ident).then_inc(s.turned, 1)
            pe.wait_ge(s.turned_copied, 1)
            for t in range(NT):
                pe.matmul(m.tiles(7)[:, t, :], tile(b.turned, t), w.exp_bo[0:E, :], start=True,
                          stop=True).then_inc(s.bias, 1)

        @block.scalar
        def _(act):
            loaded(m, act, "ffn")
            for k in range(NETS * FC):
                act.wait_ge(s.up, k + 1)
                if k >= 4:
                    act.wait_ge(s.hidden, k - 3)
                act.activation(b.grown[:, k % 4, :], m.ps[:, k % 4, :], ACT.Exp,
                               bias=w.ffn_bi[:, k:k + 1]).then_inc(s.grown, 1)
                act.activation(b.kept[:, k % 4, :], m.ps[:, k % 4, :], ACT.Relu,
                               bias=w.ffn_bi[:, k:k + 1]).then_inc(s.kept, 1)
            act.wait_ge(s.turned, NT)
            act.activation(b.turned[:, :], m.ps[0:E, 6, :], ACT.Copy).then_inc(s.turned_copied, 1)

        @block.vector
        def _(ve):
            step = Steps(ve)
            loaded(m, ve, "rows")

            def selu(k):
                ve.wait_ge(s.grown, k + 1)
                step(ve.tensor_scalar(b.grown[:, k % 4, :], b.grown[:, k % 4, :], 1.0, 1.0, ALU.min,
                                      ALU.subtract), s.fell)
                ve.wait_ge(s.kept, k + 1)
                if k >= 8:
                    ve.wait_ge(s.down, k // FC - 1)
                ve.scalar_tensor_tensor(b.hidden[:, k % 8, :], b.grown[:, k % 4, :], SELU_ALPHA,
                                        b.kept[:, k % 4, :], ALU.mult, ALU.add).then_inc(s.hidden, 1)

            def gate():
                ve.wait_ge(s.down, 1)
                step(ve.scalar_tensor_tensor(b.logits[:, :, :], m.tiles(4), SELU_SCALE, m.rows("gate_bo", NT),
                                             ALU.mult, ALU.add), s.logits)
                for t in range(NT):
                    step.tell(ve.max(b.top[:, t, :], b.logits[:, t, :]), s.top)
                ve.wait_ge(s.top, NT)
                step(ve.tensor_tensor(b.both[:, :], b.top[:, :, 0], b.top[:, :, 1], ALU.add), s.both)
                step(ve.reciprocal(b.both[:, :], b.both[:, :]), s.both)
                for t in range(NT):
                    step(ve.scalar_tensor_tensor(b.weight[:, t, :], b.logits[:, t, 0:E], b.top[:, t, 1:2],
                                                 b.logits[:, t, 0:E], ALU.is_ge, ALU.mult), s.share)
                    step(ve.tensor_scalar(b.weight[:, t, :], b.weight[:, t, :], b.both[:, t:t + 1], None,
                                          ALU.mult), s.weight)
                step(ve.tensor_scalar(b.scaled[:, :, :], b.weight[:, :, :], SELU_SCALE, None, ALU.mult), s.scaled)

            def combine(e):
                ve.wait_ge(s.down, e + 1)
                if e >= 2:
                    ve.wait_ge(s.combined, NT * (e - 1))
                for t in range(NT):
                    ve.scalar_tensor_tensor(x[:, t, :], m.tiles(4 + e % 2)[:, t, :], b.scaled[:, t, e - 1:e],
                                            x[:, t, :], ALU.mult, ALU.add).then_inc(s.combined, 1)

            for e in range(NETS):
                for f in range(FC):
                    selu(FC * e + f)
                if e == 1:
                    gate()
                if e >= 2:
                    combine(e - 1)
            combine(NETS - 1)
            ve.wait_ge(s.combined, NT * E)
            ve.wait_ge(s.bias, NT)
            step(ve.tensor_tensor(x[:, :, :], x[:, :, :], m.tiles(7), ALU.add), s.summed)


def tile_of(t):
    return slice(t * P, (t + 1) * P)



def linear_attention(m, x, tok, xT):
    w = m.w
    H, D = 16, 8
    G = NT * H
    normalize(m, x, tok, flat(xT))
    with buffers(m, inner=[P, NT, P]) as bi:
        normalize(m, tok, bi.inner, flat(xT), w.ln_g, w.ln_b, ("l0b",))
    with buffers(m, q=[P, NT, P], peak=[P, G], total=[P, G], k=[P, TOK], kpeak=[P, SEQS], ksum=[P, SEQS],
                 kt=[P, NT, P], v=[P, NT, P], qT=[P, TOK], mix=[P, SEQS, P]) as b, \
            stage(m, "q k v k_bias k_inverse q_bias peak q_low q_exp total q_share kpeak k_exp k_share turned kt qt v_done "
                     "mixed mix_done out summed") as (block, s):
        heads = lambda a: a.rearrange("p t (h d) -> p (t h) d", d=D)
        spread = lambda a: a.unsqueeze(2).to_broadcast([P, G, D])

        @block.tensor
        def _(pe):
            loaded(m, pe, "l0b")
            for t in range(NT):
                pe.matmul(m.tiles(0)[:, t, :], tile(xT, t), w.l0_wq, start=True, stop=True).then_inc(s.q, 1)
            pe.matmul(m.ps[:, 1, :], w.l0_wk, xT[:, :], start=True, stop=True).then_inc(s.k, 1)
            for t in range(NT):
                pe.matmul(m.tiles(2)[:, t, :], tile(xT, t), w.l0_wv, start=True, stop=True).then_inc(s.v, 1)
            pe.wait_ge(s.k_share, SEQS)
            for t in range(NT):
                pe.transpose(m.tiles(3)[:, t, :], tile(b.k, t), m.ident).then_inc(s.turned, 1)
            pe.wait_ge(s.q_share, 1)
            for t in range(NT):
                pe.transpose(m.tiles(4)[:, t, :], b.q[:, t, :], m.ident).then_inc(s.turned, 1)
            pe.wait_ge(s.kt, 1)
            pe.wait_ge(s.v_done, 1)
            for q in range(SEQS):
                for h in range(TPS):
                    mm = pe.matmul(m.tiles(5)[:, q, :], b.kt[:, q * TPS + h, :], b.v[:, q * TPS + h, :],
                                   start=(h == 0), stop=(h == TPS - 1))
                mm.then_inc(s.mixed, 1)
            pe.wait_ge(s.mix_done, 1)
            pe.wait_ge(s.qt, 1)
            for t in range(NT):
                pe.matmul(m.tiles(6)[:, t, :], tile(b.qT, t), b.mix[:, t // TPS, :], start=True,
                          stop=True).then_inc(s.out, 1)

        @block.scalar
        def _(act):
            act.wait_ge(s.kpeak, 1)
            for q in range(SEQS):
                r = slice(q * T, (q + 1) * T)
                act.activation(b.k[:, r], m.ps[:, 1, r], ACT.Exp, bias=b.kpeak[:, q:q + 1],
                               accum_out=b.ksum[:, q:q + 1]).then_inc(s.k_exp, 1)
            act.wait_ge(s.q_low, 1)
            act.activation(b.q[:, :, :], b.q[:, :, :], ACT.Exp).then_inc(s.q_exp, 1)
            act.wait_ge(s.turned, NT)
            act.activation(b.kt[:, :, :], m.tiles(3), ACT.Copy).then_inc(s.kt, 1)
            act.wait_ge(s.turned, 2 * NT)
            act.activation(b.qT[:, :], m.ps[:, 4, :], ACT.Copy).then_inc(s.qt, 1)

        @block.vector
        def _(ve):
            step = Steps(ve)
            loaded(m, ve, "rows")
            ve.wait_ge(s.k, 1)
            loaded(m, ve, "l0b")
            step(ve.tensor_scalar(b.k[:, :], m.ps[:, 1, :], w.l0_bk, None, ALU.add), s.k_bias)
            step(ve.tensor_reduce(b.kpeak[:, :], b.k[:, :].rearrange("p (b t) -> p b t", b=SEQS), X, ALU.max,
                                  negate=True), s.kpeak)
            ve.wait_ge(s.q, NT)
            step(ve.tensor_tensor(b.q[:, :, :], m.tiles(0), m.rows("l0_bq", NT), ALU.add), s.q_bias)
            step(ve.tensor_reduce(b.peak[:, :], heads(b.q[:, :, :]), X, ALU.max), s.peak)
            step(ve.tensor_tensor(heads(b.q[:, :, :]), heads(b.q[:, :, :]), spread(b.peak[:, :]), ALU.subtract),
                 s.q_low)
            ve.wait_ge(s.v, NT)
            step(ve.tensor_tensor(b.v[:, :, :], m.tiles(2), m.rows("l0_bv", NT), ALU.add), s.v_done)
            ve.wait_ge(s.k_exp, SEQS)
            step(ve.reciprocal(b.ksum[:, :], b.ksum[:, :]), s.k_inverse)
            for q in range(SEQS):
                r = slice(q * T, (q + 1) * T)
                step(ve.tensor_scalar(b.k[:, r], b.k[:, r], b.ksum[:, q:q + 1], None, ALU.mult), s.k_share)
            ve.wait_ge(s.q_exp, 1)
            step(ve.tensor_reduce(b.total[:, :], heads(b.q[:, :, :]), X, ALU.add), s.total)
            step(ve.reciprocal(b.total[:, :], b.total[:, :]), s.total)
            step(ve.tensor_tensor(heads(b.q[:, :, :]), heads(b.q[:, :, :]), spread(b.total[:, :]), ALU.mult),
                 s.q_share)
            ve.wait_ge(s.mixed, SEQS)
            step(ve.tensor_tensor(b.mix[:, :, :], m.tiles(5)[:, 0:SEQS, :],
                                  m.heads8.unsqueeze(1).to_broadcast([P, SEQS, P]), ALU.mult), s.mix_done)
            step(ve.tensor_tensor(x[:, :, :], x[:, :, :], tok[:, :, :], ALU.add), s.summed)
            ve.wait_ge(s.out, NT)
            step(ve.tensor_tensor(x[:, :, :], x[:, :, :], m.tiles(6), ALU.add), s.summed)



def windowed_attention(m, x, tok, xT):
    w = m.w
    CT, H, D = 8, 16, 64
    WINDOW = 64
    NEAR = P + WINDOW
    UNITS = 3 * CT
    normalize(m, x, tok, flat(xT))
    with buffers(m, qk=[P, CT, 2, TOK], v=[P, NT, H, D], inv=[P, NT, 2, H]) as b:
        with buffers(m, conv_in=[P, 2, SEQS, 3 + T], conv=[P, 3, TOK], cosed=[P, 2, TOK], sined=[P, 2, TOK],
                     square=[P, 2, TOK]) as c, \
                stage(m, "cleared projected copied begun convolved crossed cosed sined rotated squared "
                         "measured rooted inverse v_copied") as (block, s):
            lengths = m.ps[:, 4, 0:NT * 2 * H].rearrange("p (t r h) -> p t r h", t=NT, r=2)
            seqs = lambda a: a.rearrange("p (b t) -> p b t", b=SEQS)
            both = lambda a: a.unsqueeze(1).to_broadcast([P, SEQS, T])

            def rotary(k):
                return k % 3 < 2

            def qks(k):
                return 2 * (k // 3) + min(k % 3, 2)

            def vs(k):
                return k // 3

            @block.tensor
            def _(pe):
                loaded(m, pe, "l1a", "const")

                def project(k):
                    if k >= 2:
                        pe.wait_ge(s.copied, k - 1)
                    pe.matmul(m.ps[:, k % 2, :], tile(w.l1_wqkv, (k % 3) * CT + k // 3), xT[:, :], start=True,
                              stop=True).then_inc(s.projected, 1)

                def cross(k):
                    pe.wait_ge(s.convolved, 3 * (k + 1))
                    if k >= 2:
                        if rotary(k - 2):
                            pe.wait_ge(s.sined, qks(k - 2) + 1)
                        else:
                            pe.wait_ge(s.v_copied, vs(k - 2) + 1)
                    if rotary(k):
                        pe.matmul(m.ps[:, 2 + k % 2, :], m.w.half_turn, c.conv[:, k % 3, :], start=True,
                                  stop=True).then_inc(s.crossed, 1)
                    else:
                        for t in range(NT):
                            mm = pe.transpose(m.tiles(2 + k % 2)[:, t, :], tile(c.conv[:, k % 3, :], t), m.ident)
                        mm.then_inc(s.crossed, 1)

                def measure(k):
                    if not rotary(k):
                        return
                    n = qks(k)
                    pe.wait_ge(s.squared, n + 1)
                    for t in range(NT):
                        mm = pe.matmul(lengths[:, t, k % 3, 2 * (k // 3):2 * (k // 3) + 2],
                                       tile(c.square[:, n % 2, :], t), m.w.heads64[:, 0:P:D], start=True, stop=True)
                    mm.then_inc(s.measured, 1)

                project(0)
                for k in range(UNITS + 4):
                    if k + 1 < UNITS:
                        project(k + 1)
                    if 1 <= k <= UNITS:
                        cross(k - 1)
                    if k >= 4:
                        measure(k - 4)

            @block.scalar
            def _(act):
                loaded(m, act, "l1a")

                def copy(k):
                    act.wait_ge(s.projected, k + 1)
                    act.wait_ge(s.cleared, 1)
                    if k >= 2:
                        act.wait_ge(s.convolved, 3 * (k - 1))
                    j = (k % 3) * CT + k // 3
                    act.activation(c.conv_in[:, k % 2, :, 3:], m.ps[:, k % 2, :].rearrange("p (b t) -> p b t", b=SEQS),
                                   ACT.Identity, bias=w.l1_bqkv[:, j:j + 1]).then_inc(s.copied, 1)
                    act.wait_ge(s.copied, k + 1)
                    if k >= 3:
                        act.wait_ge(s.crossed, k - 2)
                        if qks(k - 2):
                            act.wait_ge(s.cosed, qks(k - 2))
                    act.activation(seqs(c.conv[:, k % 3, :]), c.conv_in[:, k % 2, :, 0:T], ACT.Identity,
                                   bias=w.l1_tap_bias[:, j:j + 1], scale=w.l1_taps[:, 4 * j:4 * j + 1]
                                   ).then_inc(s.begun, 1)

                def square(k):
                    if rotary(k):
                        n = qks(k)
                        act.wait_ge(s.rotated, n + 1)
                        if n >= 2:
                            act.wait_ge(s.measured, n - 1)
                        act.activation(c.square[:, n % 2, :], b.qk[:, k // 3, k % 3, :],
                                       ACT.Square).then_inc(s.squared, 1)
                    else:
                        act.wait_ge(s.crossed, k + 1)
                        act.activation(b.v[:, :, 2 * (k // 3):2 * (k // 3) + 2, 0:D],
                                       m.ps[:, 2 + k % 2, :].rearrange("p (t h d) -> p t h d", t=NT, h=2),
                                       ACT.Copy).then_inc(s.v_copied, 1)

                copy(0)
                for k in range(UNITS + 3):
                    if k + 1 < UNITS:
                        copy(k + 1)
                    if 2 <= k < UNITS + 2 and not rotary(k - 2):
                        square(k - 2)
                    if k >= 3 and rotary(k - 3):
                        square(k - 3)
                act.wait_ge(s.measured, 2 * CT)
                act.activation(b.inv[:, :, :, :], lengths, ACT.Sqrt, bias=m.w.tiny[:, 0:1]).then_inc(s.rooted, 1)

            @block.vector
            def _(ve):
                step = Steps(ve)
                loaded(m, ve, "l1a", "const")
                step(ve.memset(c.conv_in[:, :, :, 0:3], 0.0), s.cleared)

                def convolve(k, i):
                    j = (k % 3) * CT + k // 3
                    if i == 1:
                        ve.wait_ge(s.begun, k + 1)
                    else:
                        ve.wait_ge(s.convolved, 3 * k + i - 1)
                    out = seqs(c.conv[:, k % 3, :])
                    ve.scalar_tensor_tensor(out, c.conv_in[:, k % 2, :, i:i + T], w.l1_taps[:, 4 * j + i:4 * j + i + 1],
                                            out, ALU.mult, ALU.add).then_inc(s.convolved, 1)

                def rotate(k):
                    ve.wait_ge(s.crossed, k + 1)
                    if qks(k) >= 2:
                        ve.wait_ge(s.rotated, qks(k) - 1)
                    ve.tensor_tensor(seqs(c.sined[:, qks(k) % 2, :]), seqs(m.ps[:, 2 + k % 2, :]), both(m.w.sine), ALU.mult
                                     ).then_inc(s.sined, 1)

                for k in range(UNITS + 1):
                    turning = k >= 2 and rotary(k - 2)
                    if k < UNITS:
                        convolve(k, 1)
                    if turning:
                        rotate(k - 2)
                    if k < UNITS:
                        convolve(k, 2)
                    if k < UNITS:
                        convolve(k, 3)
                ve.wait_ge(s.rooted, 1)
                step(ve.reciprocal(b.inv[:, :, :, :], b.inv[:, :, :, :]), s.inverse)
                step(ve.tensor_scalar(b.inv[:, :, 1, :], b.inv[:, :, 1, :], float(D) ** -0.5, None, ALU.mult),
                     s.inverse)

            @block.gpsimd
            def _(po):
                loaded(m, po, "const")
                for k in range(UNITS + 2):
                    if k < UNITS and rotary(k):
                        n = qks(k)
                        po.wait_ge(s.convolved, 3 * (k + 1))
                        if n >= 2:
                            po.wait_ge(s.rotated, n - 1)
                        po.tensor_tensor(seqs(c.cosed[:, n % 2, :]), seqs(c.conv[:, k % 3, :]), both(m.w.cosine),
                                         ALU.mult).then_inc(s.cosed, 1)
                    if k >= 2 and rotary(k - 2):
                        n = qks(k - 2)
                        po.wait_ge(s.sined, n + 1)
                        po.wait_ge(s.cosed, n + 1)
                        po.tensor_tensor(b.qk[:, (k - 2) // 3, (k - 2) % 3, :], c.sined[:, n % 2, :],
                                         c.cosed[:, n % 2, :], ALU.add).then_inc(s.rotated, 1)

        with buffers(m, probs=[P, 3, 2, NEAR + P], q_apart=[P, 2, 2, TOK], q_scale=[H, TOK], pick=[H, CT * P],
                     ones=[P, D], inverse=[P, T], oT=[P, 2, TOK]) as c, \
                stage(m, "ready turned scale_kept spread apart scores exps masked mixed inverse normed "
                         "projected kept back biased summed") as (block, s):
            UNITS = CT * SEQS

            @block.tensor
            def _(pe):
                for t in range(NT):
                    mm = pe.transpose(m.ps[0:H, 7, tile_of(t)], b.inv[:, t, 0, :], m.ident)
                mm.then_inc(s.turned, 1)
                pe.wait_ge(s.ready, 2)
                pe.wait_ge(s.scale_kept, 1)

                def spread(g):
                    if g >= 1:
                        pe.wait_ge(s.apart, 2 * g)
                    pe.matmul(m.ps[:, 7, :], tile(c.pick, g), c.q_scale[:, :], start=True, stop=True
                              ).then_inc(s.spread, 1)

                def score(u):
                    g, at = u // SEQS, (u % SEQS) * T
                    pe.wait_ge(s.apart, 2 * (g + 1))
                    if u >= 2:
                        pe.wait_ge(s.exps, 4 * (u - 1))
                    bank = 2 * (u % 2)
                    pe.matmul(m.ps[:, bank, 0:2 * NEAR], b.qk[:, g, 1, at:at + P],
                              c.q_apart[:, g % 2, :, at:at + NEAR], start=True, stop=True)
                    pe.matmul(m.ps[:, bank + 1, 0:2 * P], b.qk[:, g, 1, at + P:at + T],
                              c.q_apart[:, g % 2, :, at + P:at + T], start=True, stop=True).then_inc(s.scores, 1)

                def mix(u):
                    g, q = u // SEQS, u % SEQS
                    pe.wait_ge(s.masked, u + 1)
                    if u >= 2:
                        pe.wait_ge(s.normed, u - 1)
                    for part in range(2):
                        for j in range(2):
                            pr = c.probs[:, u % 3, j, :]
                            left = [c.ones[:, :] if part else b.v[:, TPS * q + i, 2 * g + j, :] for i in range(TPS)]
                            out = m.ps[D * j:D * j + D, 4 + u % 2, part * T:part * T + T]
                            for o_, l_, r_, first in ((out[:, 0:P], left[0], pr[:, 0:P], True),
                                                      (out[:, P:T], left[1], pr[:, NEAR:NEAR + P], True),
                                                      (out[:, P:NEAR], left[0], pr[:, P:NEAR], False)):
                                mm = pe.matmul(o_, l_, r_, start=first, stop=True, tile_position=(0, D * j),
                                               skip_group_check=True)
                    mm.then_inc(s.mixed, 1)

                def project(g):
                    pe.wait_ge(s.normed, SEQS * (g + 1))
                    pe.matmul(m.ps[:, 6, :], tile(w.l1_wo, g), c.oT[:, g % 2, :], start=(g == 0),
                              stop=(g == CT - 1)).then_inc(s.projected, 1)

                spread(0)
                spread(1)
                for u in range(UNITS + 6):
                    if u >= 2 and u % 2 == 0 and u // 2 + 1 < CT:
                        spread(u // 2 + 1)
                    if u < UNITS:
                        score(u)
                    if 2 <= u < UNITS + 2:
                        mix(u - 2)
                    if u >= 6 and u % 2 == 0:
                        project((u - 6) // 2)
                pe.wait_ge(s.kept, 1)
                for t in range(NT):
                    mm = pe.transpose(m.tiles(7)[:, t, :], tile(c.q_apart[:, 0, 0, :], t), m.ident)
                mm.then_inc(s.back, 1)

            @block.scalar
            def _(act):
                act.wait_ge(s.turned, 1)
                act.activation(c.q_scale[:, :], m.ps[0:H, 7, :], ACT.Copy).then_inc(s.scale_kept, 1)
                for u in range(UNITS):
                    g, q = u // SEQS, u % SEQS
                    act.wait_ge(s.scores, u + 1)
                    if u >= 3:
                        act.wait_ge(s.mixed, u - 2)
                    for j in range(2):
                        for i, (n, at) in enumerate(((NEAR, 0), (P, NEAR))):
                            act.activation(c.probs[:, u % 3, j, at:at + n],
                                           m.ps[:, 2 * (u % 2) + i, j * n:j * n + n], ACT.Exp,
                                           scale=b.inv[:, TPS * q + i, 1, 2 * g + j:2 * g + j + 1]).then_inc(s.exps, 1)
                act.wait_ge(s.projected, CT)
                act.activation(c.q_apart[:, 0, 0, :], m.ps[:, 6, :], ACT.Copy).then_inc(s.kept, 1)

            @block.gpsimd
            def _(po):
                po.memset(c.ones[:, :], 1.0).then_inc(s.ready, 1)
                for u in range(UNITS):
                    po.wait_ge(s.exps, 4 * (u + 1))
                    po.tensor_tensor(c.probs[:, u % 3, :, :], c.probs[:, u % 3, :, :],
                                     m.w.band.unsqueeze(1).to_broadcast([P, 2, NEAR + P]),
                                     ALU.mult).then_inc(s.masked, 1)

            @block.vector
            def _(ve):
                step = Steps(ve)
                loaded(m, ve, "rows")
                ve.tensor_copy(c.pick[:, :].rearrange("p (h d) -> p h d", d=D),
                               m.ident[0:H, 0:H].unsqueeze(2).to_broadcast([H, H, D])).then_inc(s.ready, 1)
                step(ve.tensor_tensor(x[:, :, :], x[:, :, :], m.rows("l1_bo", NT), ALU.add), s.biased)

                def apart(g):
                    ve.wait_ge(s.spread, g + 1)
                    if g >= 2:
                        ve.wait_ge(s.scores, SEQS * (g - 1))
                    for j in range(2):
                        ve.scalar_tensor_tensor(c.q_apart[:, g % 2, j, :], m.ps[:, 7, :], m.w.heads64[:, D * j:D * j + 1],
                                                b.qk[:, g, 0, :], ALU.mult, ALU.mult).then_inc(s.apart, 1)

                def norm(u):
                    g, at = u // SEQS, (u % SEQS) * T
                    ve.wait_ge(s.mixed, u + 1)
                    step(ve.reciprocal(c.inverse[:, :], m.ps[:, 4 + u % 2, T:2 * T]), s.inverse)
                    if g >= 2:
                        ve.wait_ge(s.projected, g - 1)
                    step(ve.tensor_tensor(c.oT[:, g % 2, at:at + T], m.ps[:, 4 + u % 2, 0:T], c.inverse[:, :],
                                          ALU.mult), s.normed)

                apart(0)
                apart(1)
                for g in range(CT):
                    if g + 2 < CT:
                        apart(g + 2)
                    norm(2 * g)
                    norm(2 * g + 1)
                ve.wait_ge(s.back, 1)
                step(ve.tensor_tensor(x[:, :, :], x[:, :, :], m.tiles(7), ALU.add), s.summed)



def channel_mix(m, x, tok, xT):
    w = m.w
    with buffers(m, shifted=[P, SEQS, 1 + T], xr=[P, TOK], xk=[P, TOK], rest=[P, 2], gate=[P, NT, P],
                 k=[P, TOK], y=[P, NT, P]) as b:
        normalize(m, x, tok, padded(b.shifted, 1))
        with stage(m, "cleared rest part mixed r k relued squared gated v y summed") as (block, s):
            @block.vector
            def _(ve):
                step = Steps(ve)
                loaded(m, ve, "l1f")
                step(ve.memset(b.shifted[:, :, 0:1], 0.0), s.cleared)
                step(ve.tensor_scalar(b.rest[:, :], w.mu, -1.0, 1.0, ALU.mult, ALU.add), s.rest)
                for j, out in enumerate((b.xk, b.xr)):
                    o = out[:, :].rearrange("p (b t) -> p b t", b=SEQS)
                    step(ve.tensor_scalar(o, b.shifted[:, :, 0:T], b.rest[:, j:j + 1], None, ALU.mult), s.part)
                    step(ve.scalar_tensor_tensor(o, b.shifted[:, :, 1:], w.mu[:, j:j + 1], o, ALU.mult, ALU.add),
                         s.mixed)
                ve.wait_ge(s.gated, 1)
                ve.wait_ge(s.v, 1)
                step(ve.tensor_tensor(b.y[:, :, :], m.tiles(2), b.gate[:, :, :], ALU.mult), s.y)
                step(ve.tensor_tensor(x[:, :, :], x[:, :, :], b.y[:, :, :], ALU.add), s.summed)

            @block.tensor
            def _(pe):
                loaded(m, pe, "l1f")
                pe.wait_ge(s.mixed, 1)
                pe.matmul(m.ps[:, 0, :], w.l1_wk, b.xk[:, :], start=True, stop=True).then_inc(s.k, 1)
                pe.wait_ge(s.mixed, 2)
                for t in range(NT):
                    mm = pe.matmul(m.tiles(1)[:, t, :], tile(b.xr, t), w.l1_wr, start=True, stop=True)
                mm.then_inc(s.r, 1)
                pe.wait_ge(s.squared, 1)
                for t in range(NT):
                    mm = pe.matmul(m.tiles(2)[:, t, :], tile(b.k, t), w.l1_wv, start=True, stop=True)
                mm.then_inc(s.v, 1)

            @block.scalar
            def _(act):
                act.wait_ge(s.k, 1)
                act.activation(b.k[:, :], m.ps[:, 0, :], ACT.Relu).then_inc(s.relued, 1)
                act.wait_ge(s.relued, 1)
                act.activation(b.k[:, :], b.k[:, :], ACT.Square).then_inc(s.squared, 1)
                act.wait_ge(s.r, 1)
                act.activation(b.gate[:, :, :], m.tiles(1), ACT.Sigmoid).then_inc(s.gated, 1)



def delta_rule(m, x, tok, xT):
    w = m.w
    H, D, CH = 4, 32, 32
    LONG, SHORT = 64, 5
    PAD = LONG - 1
    PER = P // CH
    BY_PE, BY_VECTOR = 16, 30
    RING = 4
    G = NT * H
    normalize(m, x, tok, flat(xT))
    with buffers(m, src=[P, 4, NT, P]) as o:
        with buffers(m, conv_in=[P, 3, SEQS, 3 + T], qkT=[P, 2, TOK], v_in=[P, SEQS, PAD + T],
                     short=[P, TOK], long=[P, TOK], qk=[P, 2, NT, P], kb=[P, NT, P], beta=[P, G],
                     y=[P, NT, H, 2 * D], qn=[P, TOK], kn=[P, TOK], kbn=[P, TOK]) as b:
            with buffers(m, conv=[P, 3, TOK], square=[P, 2, NT, P], norm=[P, 2 * G], shifted=[P, 2 * G],
                         root=[P, 2 * G], scaled=[P, RING, P]) as c, \
                    stage(m, "projected copied cleared convolved active v_active beta_made beta_open beta "
                             "shorts longs scaled filtered turned taken squared sums shifted root normed kb vb turned_again "
                             "taken_again turned_f taken_f") as (block, s):
                @block.tensor
                def _(pe):
                    loaded(m, pe, "l1b", "const")
                    for r in range(3):
                        pe.matmul(m.ps[:, r, :], tile(w.d_wqkv, r), xT[:, :], start=True, stop=True
                                  ).then_inc(s.projected, 1)
                    for t in range(NT):
                        mm = pe.matmul(m.ps[:, 3, H * t:H * t + H], tile(xT, t), w.d_wb, start=True, stop=True)
                    mm.then_inc(s.beta_made, 1)
                    for r in range(2):
                        pe.wait_ge(s.active, r + 1)
                        for t in range(NT):
                            mm = pe.transpose(m.tiles(4 + r)[:, t, :], tile(b.qkT[:, r, :], t), m.ident)
                        mm.then_inc(s.turned, 1)
                    pe.wait_ge(s.v_active, 1)
                    for t in range(NT):
                        at = PAD + (t % TPS) * P
                        mm = pe.transpose(m.tiles(6)[:, t, :], b.v_in[:, t // TPS, at:at + P], m.ident)
                    mm.then_inc(s.turned, 1)
                    for i in range(BY_PE):
                        pe.wait_ge(s.scaled, i + 1)
                        pe.matmul(m.ps[:, 7, :], c.scaled[:, i % RING, :], b.v_in[:, :, i:i + T], start=(i == 0),
                                  stop=(i == BY_PE - 1)).then_inc(s.filtered, 1)
                    for r in range(3):
                        if r == 0:
                            pe.wait_ge(s.normed, 1)
                        elif r == 1:
                            pe.wait_ge(s.normed, 2)
                        else:
                            pe.wait_ge(s.kb, 1)
                        for t in range(NT):
                            tokens = b.qk[:, r, t, :] if r < 2 else b.kb[:, t, :]
                            mm = pe.transpose(m.tiles(r)[:, t, :], tokens, m.ident)
                        mm.then_inc(s.turned_again, 1)
                    pe.wait_ge(s.shorts, SHORT)
                    pe.wait_ge(s.taken, 3)
                    for t in range(NT):
                        mm = pe.transpose(m.tiles(4)[:, t, :], tile(b.short, t), m.ident)
                    mm.then_inc(s.turned_f, 1)

                @block.scalar
                def _(act):
                    for r in range(3):
                        act.wait_ge(s.projected, r + 1)
                        act.activation(c_in(b, r), m.ps[:, r, :].rearrange("p (b t) -> p b t", b=SEQS),
                                       ACT.Copy).then_inc(s.copied, 1)
                    act.wait_ge(s.cleared, 2)
                    for r in range(3):
                        act.wait_ge(s.convolved, 4 * (r + 1))
                        if r < 2:
                            act.activation(b.qkT[:, r, :], c.conv[:, r, :], ACT.Silu).then_inc(s.active, 1)
                        else:
                            act.activation(b.v_in[:, :, PAD:], c.conv[:, r, :].rearrange("p (b t) -> p b t", b=SEQS),
                                           ACT.Silu).then_inc(s.v_active, 1)
                    act.wait_ge(s.beta_made, 1)
                    act.activation(b.beta[:, :], m.ps[:, 3, 0:G], ACT.Sigmoid).then_inc(s.beta_open, 1)
                    for r in range(2):
                        act.wait_ge(s.turned, r + 1)
                        act.activation(b.qk[:, r, :, :], m.tiles(4 + r), ACT.Copy).then_inc(s.taken, 1)
                    act.wait_ge(s.turned, 3)
                    act.activation(o.src[:, 3, :, :], m.tiles(6), ACT.Copy).then_inc(s.taken, 1)
                    act.wait_ge(s.taken, 2)
                    act.activation(c.square[:, :, :, :], b.qk[:, :, :, :], ACT.Square).then_inc(s.squared, 1)
                    loaded(m, act, "l1b", "const")
                    for i in range(BY_PE):
                        if i >= RING:
                            act.wait_ge(s.filtered, i - RING + 1)
                        act.activation(c.scaled[:, i % RING, :], m.ident, ACT.Copy, scale=w.d_long[:, i:i + 1]
                                       ).then_inc(s.scaled, 1)
                    for r, out in enumerate((b.qn, b.kn, b.kbn)):
                        act.wait_ge(s.turned_again, r + 1)
                        act.activation(out[:, :], m.ps[:, r, :], ACT.Copy).then_inc(s.taken_again, 1)
                    act.wait_ge(s.turned_f, 1)
                    act.activation(o.src[:, 0, :, :], m.tiles(4), ACT.Copy).then_inc(s.taken_f, 1)

                @block.vector
                def _(ve):
                    step = Steps(ve)
                    loaded(m, ve, "l1b")
                    step(ve.memset(b.conv_in[:, :, :, 0:3], 0.0), s.cleared)
                    step(ve.memset(b.v_in[:, :, 0:PAD], 0.0), s.cleared)
                    for r in range(3):
                        ve.wait_ge(s.copied, r + 1)
                        out = c.conv[:, r, :].rearrange("p (b t) -> p b t", b=SEQS)
                        step(ve.tensor_scalar(out, b.conv_in[:, r, :, 0:T], w.d_taps[:, 4 * r:4 * r + 1], None,
                                              ALU.mult), s.convolved)
                        for i in range(1, 4):
                            step(ve.scalar_tensor_tensor(out, b.conv_in[:, r, :, i:i + T],
                                                         w.d_taps[:, 4 * r + i:4 * r + i + 1], out,
                                                         ALU.mult, ALU.add), s.convolved)
                    ve.wait_ge(s.beta_open, 1)
                    step(ve.tensor_scalar(b.beta[:, :], b.beta[:, :], 1e-6, None, ALU.max), s.beta)
                    ve.wait_ge(s.squared, 1)
                    step(ve.tensor_reduce(c.norm[:, :], c.square[:, :, :, :].rearrange(
                        "p r t (h d) -> p (r t h) d", d=D), X, ALU.add), s.sums)
                    ve.wait_ge(s.v_active, 1)

                    def fir(out, taps, n, sem, first, last):
                        o_ = out[:, :].rearrange("p (b t) -> p b t", b=SEQS)
                        for i in range(first, last):
                            v_ = b.v_in[:, :, PAD - n + 1 + i:PAD - n + 1 + i + T]
                            if i == first:
                                step(ve.tensor_scalar(o_, v_, taps[:, i:i + 1], None, ALU.mult), sem)
                            else:
                                step(ve.scalar_tensor_tensor(o_, v_, taps[:, i:i + 1], o_, ALU.mult, ALU.add), sem)

                    fir(b.short, w.d_short, SHORT, s.shorts, 0, SHORT)
                    ve.wait_ge(s.root, 1)
                    for r in range(2):
                        qk = b.qk[:, r, :, :].rearrange("p t (h d) -> p (t h) d", d=D)
                        step(ve.tensor_tensor(qk, qk, c.root[:, G * r:G * r + G].unsqueeze(2).to_broadcast([P, G, D]),
                                              ALU.mult), s.normed)
                    beta = b.beta[:, :].unsqueeze(2).to_broadcast([P, G, D])
                    step(ve.tensor_tensor(b.kb[:, :, :].rearrange("p t (h d) -> p (t h) d", d=D),
                                          b.qk[:, 1, :, :].rearrange("p t (h d) -> p (t h) d", d=D), beta, ALU.mult),
                         s.kb)
                    y = b.y[:, :, :, :].rearrange("p t h d -> p (t h) d")
                    ve.wait_ge(s.taken, 3)
                    step(ve.tensor_tensor(y[:, :, 0:D], o.src[:, 3, :, :].rearrange("p t (h d) -> p (t h) d", d=D),
                                          beta, ALU.mult), s.vb)
                    step(ve.tensor_copy(y[:, :, D:2 * D], b.kb[:, :, :].rearrange("p t (h d) -> p (t h) d", d=D)),
                         s.vb)

                    fir(b.long, w.d_long, LONG, s.longs, BY_PE, BY_VECTOR)
                    ve.wait_ge(s.filtered, BY_PE)
                    step(ve.tensor_tensor(b.long[:, :], b.long[:, :], m.ps[:, 7, :], ALU.add), s.longs)

                @block.gpsimd
                def _(po):
                    po.wait_ge(s.sums, 1)
                    po.tensor_scalar(c.shifted[:, :], c.norm[:, :], 1e-6, None, ALU.add).then_inc(s.shifted, 1)
                    po.wait_ge(s.shifted, 1)
                    po.tensor_tensor(c.root[:, :], c.shifted[:, :], m.minus_half[:, 0:2 * G],
                                     ALU.pow).then_inc(s.root, 1)

            LEVELS = 5
            with buffers(m, mixT=[P, NT, H, P]) as mix:
                def nth(t, i, levels):
                    return (t // 2) * 2 * levels + 2 * i + t % 2 + 1

                applied_bank, turned_bank, power_bank = (6, 1), (4, 7), (5, 0)
                with buffers(m, n=[P, 2, 2, H, P], nT=[P, 2, 2, H, P], product=[P, RING, SEQS, T]) as c, \
                        stage(m, "low_kept high_kept mix mix_kept applied added squaredT squaredT_kept "
                                 "squared squared_kept product long") as (block, s):
                    @block.tensor
                    def _(pe):
                        def products(t):
                            if t == 2:
                                pe.wait_ge(s.added, nth(1, LEVELS - 1, LEVELS))
                                pe.wait_ge(s.squared_kept, nth(1, LEVELS - 3, LEVELS - 2))
                                pe.wait_ge(s.squaredT_kept, nth(1, LEVELS - 2, LEVELS - 1))
                            for k, (left, right) in enumerate(((b.kbn, b.kn), (b.kn, b.kbn), (b.kn, b.qn))):
                                for h in range(H):
                                    r = slice(D * h, D * h + D)
                                    mm = pe.matmul(m.ps[:, H * (t % 2) + h, k * P:(k + 1) * P], left[r, tile_of(t)],
                                                   right[r, tile_of(t)], start=True, stop=True,
                                                   tile_position=(D * h, 0))
                            mm.then_inc(s.mix, 1)

                        def level(t, i):
                            if i == 0:
                                pe.wait_ge(s.low_kept, t + 1)
                                pe.wait_ge(s.high_kept, t + 1)
                                pe.wait_ge(s.mix_kept, t + 1)
                                if t % 2 == 0:
                                    pe.wait_ge(s.low_kept, t + 2)
                                    pe.wait_ge(s.high_kept, t + 2)
                                    pe.wait_ge(s.mix_kept, t + 2)
                            else:
                                pe.wait_ge(s.squaredT_kept, nth(t, i - 1, LEVELS - 1))
                                pe.wait_ge(s.added, nth(t, i - 1, LEVELS))
                            n, nT = c.n[:, t % 2, i % 2, :, :], c.nT[:, t % 2, i % 2, :, :]
                            for h in range(H):
                                mm = pe.matmul(m.ps[:, applied_bank[t % 2], 2 * D * h:2 * D * h + 2 * D], nT[:, h, :],
                                               b.y[:, t, h, :], start=True, stop=True)
                            mm.then_inc(s.applied, 1)
                            if i == LEVELS - 1:
                                return
                            if i >= 1:
                                pe.wait_ge(s.squared_kept, nth(t, i - 1, LEVELS - 2))
                            for h in range(H):
                                mm = pe.matmul(m.tiles(turned_bank[t % 2])[:, h, :], n[:, h, :], nT[:, h, :],
                                               start=True, stop=True)
                            mm.then_inc(s.squaredT, 1)
                            if i == LEVELS - 2:
                                return
                            for h in range(H):
                                mm = pe.matmul(m.tiles(power_bank[t % 2])[:, h, :], nT[:, h, :], n[:, h, :],
                                               start=True, stop=True)
                            mm.then_inc(s.squared, 1)

                        for pair in range(NT // 2):
                            products(2 * pair)
                            products(2 * pair + 1)
                            for i in range(LEVELS):
                                level(2 * pair, i)
                                level(2 * pair + 1, i)

                    @block.scalar
                    def _(act):
                        done = 0
                        for pair in range(NT // 2):
                            for i in range(LEVELS - 1):
                                for t in (2 * pair, 2 * pair + 1):
                                    act.wait_ge(s.squaredT, nth(t, i, LEVELS - 1))
                                    act.activation(c.nT[:, t % 2, (i + 1) % 2, :, :], m.tiles(turned_bank[t % 2]),
                                                   ACT.Copy).then_inc(s.squaredT_kept, 1)
                                    until = (LONG - BY_VECTOR) * nth(t, i, LEVELS - 1) // (NT * (LEVELS - 1))
                                    for k in range(done, until):
                                        if k >= RING:
                                            act.wait_ge(s.long, k - RING + 1)
                                        act.activation(c.product[:, k % RING, :, :],
                                                       b.v_in[:, :, BY_VECTOR + k:BY_VECTOR + k + T], ACT.Copy,
                                                       scale=w.d_long[:, BY_VECTOR + k:BY_VECTOR + k + 1]
                                                       ).then_inc(s.product, 1)
                                    done = until

                    @block.vector
                    def _(ve):
                        spread = lambda a: a.unsqueeze(1).to_broadcast([P, H, P])
                        for pair in range(NT // 2):
                            for t in (2 * pair, 2 * pair + 1):
                                if pair:
                                    ve.wait_ge(s.applied, nth(2 * pair - 1, LEVELS - 1, LEVELS))
                                ve.wait_ge(s.mix, t + 1)
                                ve.tensor_tensor(c.n[:, t % 2, 0, :, :], m.ps[:, H * (t % 2):H * (t % 2) + H, 0:P], spread(m.w.minus_low),
                                                 ALU.mult).then_inc(s.low_kept, 1)
                                ve.tensor_tensor(c.nT[:, t % 2, 0, :, :], m.ps[:, H * (t % 2):H * (t % 2) + H, P:2 * P], spread(m.w.minus_high),
                                                 ALU.mult).then_inc(s.high_kept, 1)
                                ve.tensor_tensor(mix.mixT[:, t, :, :], m.ps[:, H * (t % 2):H * (t % 2) + H, 2 * P:3 * P], spread(m.w.upto),
                                                 ALU.mult).then_inc(s.mix_kept, 1)
                            for i in range(LEVELS):
                                for t in (2 * pair, 2 * pair + 1):
                                    ve.wait_ge(s.applied, nth(t, i, LEVELS))
                                    if i:
                                        ve.wait_ge(s.added, nth(t, i - 1, LEVELS))
                                    ve.tensor_tensor(b.y[:, t, :, :], b.y[:, t, :, :],
                                                     m.ps[:, applied_bank[t % 2], 0:2 * D * H].rearrange(
                                                         "p (h d) -> p h d", h=H), ALU.add).then_inc(s.added, 1)
                                    if i < LEVELS - 2:
                                        ve.wait_ge(s.squared, nth(t, i, LEVELS - 2))
                                        ve.tensor_copy(c.n[:, t % 2, (i + 1) % 2, :, :], m.tiles(power_bank[t % 2])
                                                       ).then_inc(s.squared_kept, 1)

                    @block.gpsimd
                    def _(po):
                        step = Steps(po)
                        long = b.long[:, :].rearrange("p (b t) -> p b t", b=SEQS)
                        for k in range(LONG - BY_VECTOR):
                            po.wait_ge(s.product, k + 1)
                            step(po.tensor_tensor(long, long, c.product[:, k % RING, :, :], ALU.add), s.long)

                chunk_scan(m, b, mix, o, H, D, CH, PER)
        gate_sources(m, x, xT, o, H, D)


def c_in(b, r):
    return b.conv_in[:, r, :, 3:]


def chunk_scan(m, b, c, o, H, D, CH, PER):
    CHUNKS = T // CH
    with buffers(m, w_tok=[P, NT, P], wT=[P, TOK], adj=[P, NT, P], state=[P, SEQS, P], qs=[P, NT, P]) as e, \
            stage(m, "w_tok turned long_turned long_kept wT ws adj qs gain state mixed qs_kept out") as (block, s):
        @block.tensor
        def _(pe):
            for t in range(NT):
                pe.wait_ge(s.w_tok, 1)
                mm = pe.transpose(m.tiles(7)[:, t, :], e.w_tok[:, t, :], m.ident)
            mm.then_inc(s.turned, 1)
            for t in range(NT):
                mm = pe.transpose(m.tiles(6)[:, t, :], tile(b.long, t), m.ident)
            mm.then_inc(s.long_turned, 1)
            pe.wait_ge(s.wT, 1)
            for i in range(CHUNKS):
                r = slice(CH * (i % PER), CH * (i % PER) + CH)
                for q in range(SEQS):
                    at = q * T + i * CH
                    n = SEQS * i + q
                    pe.wait_ge(s.state, SEQS * i + q + 1)
                    pe.matmul(m.ps[r, q, 0:P], e.wT[:, at:at + CH], e.state[:, q, :], start=True, stop=True,
                              tile_position=(0, CH * (i % PER))).then_inc(s.ws, 1)
                    mm = pe.matmul(m.tiles(2 + q)[r, i // PER, :], b.qn[:, at:at + CH], e.state[:, q, :], start=True,
                                   stop=True, tile_position=(0, CH * (i % PER)))
                    mm.then_inc(s.qs, 1)
                for q in range(SEQS):
                    t = q * TPS + i // PER
                    pe.wait_ge(s.adj, SEQS * i + q + 1)
                    if i == CHUNKS - 1:
                        continue
                    pe.matmul(m.ps[:, 4 + q, 0:P], b.qk[r, 1, t, :], e.adj[r, t, :], start=(i == 0), stop=True,
                              tile_position=(CH * (i % PER), 0), skip_group_check=True).then_inc(s.gain, 1)
            pe.wait_ge(s.long_kept, 1)
            for t in range(NT):
                for h in range(H):
                    mm = pe.matmul(m.tiles(6)[:, t, D * h:D * h + D], c.mixT[:, t, h, :],
                                   e.adj[:, t, D * h:D * h + D], start=True, stop=True)
            mm.then_inc(s.mixed, 1)

        @block.vector
        def _(ve):
            step = Steps(ve)
            step(ve.tensor_copy(e.w_tok[:, :, :].rearrange("p t (h d) -> p (t h) d", d=D),
                                b.y[:, :, :, D:2 * D].rearrange("p t h d -> p (t h) d")), s.w_tok)
            for q in range(SEQS):
                ve.memset(e.state[:, q, :], 0.0).then_inc(s.state, 1)
            for i in range(CHUNKS):
                r = slice(CH * (i % PER), CH * (i % PER) + CH)
                for q in range(SEQS):
                    t = q * TPS + i // PER
                    ve.wait_ge(s.ws, SEQS * i + q + 1)
                    ve.tensor_tensor(e.adj[r, t, :].rearrange("p (h d) -> p h d", h=H), b.y[r, t, :, 0:D],
                                     m.ps[r, q, 0:P].rearrange("p (h d) -> p h d", h=H), ALU.subtract
                                     ).then_inc(s.adj, 1)
                if i == CHUNKS - 1:
                    continue
                for q in range(SEQS):
                    ve.wait_ge(s.gain, SEQS * i + q + 1)
                    ve.wait_ge(s.qs, SEQS * i + q + 1)
                    ve.tensor_tensor(e.state[:, q, :], m.ps[:, 4 + q, 0:P], m.w.heads32, ALU.mult
                                     ).then_inc(s.state, 1)
            ve.wait_ge(s.mixed, 1)
            ve.wait_ge(s.qs_kept, SEQS)
            step(ve.tensor_tensor(o.src[:, 2, :, :], e.qs[:, :, :], m.tiles(6), ALU.add), s.out)

        @block.scalar
        def _(act):
            act.wait_ge(s.turned, 1)
            act.activation(e.wT[:, :], m.ps[:, 7, :], ACT.Copy).then_inc(s.wT, 1)
            act.wait_ge(s.long_turned, 1)
            act.activation(o.src[:, 1, :, :], m.tiles(6), ACT.Copy).then_inc(s.long_kept, 1)
            act.wait_ge(s.qs, SEQS * CHUNKS)
            for q in range(SEQS):
                act.activation(e.qs[:, q * TPS:(q + 1) * TPS, :], m.tiles(2 + q)[:, 0:TPS, :], ACT.Copy
                               ).then_inc(s.qs_kept, 1)


def gate_sources(m, x, xT, o, H, D):
    w = m.w
    G = NT * H
    S = 4
    with buffers(m, mean=[P, S, G], centred=[P, S, G, D], square=[P, S, G, D], square0=[P, S, G, D],
                 stat=[P, NT, H, S * S], statT=[H * S * S, TOK], hidden=[P, H, TOK], logit=[P, G, S],
                 peak=[P, G], total=[P, G], mixed=[P, G, D], sq=[P, G], rms=[P, G],
                 oT=[P, TOK]) as b, \
            stage(m, "mean mean_kept size squared centred square2 l2_in l2 var turned turned_copied up hidden "
                     "down logit low exps floored product mix osq orms oroot normed "
                     "oturned ocopied out summed") as (block, s):
        groups_ = o.src[:, :, :, :].rearrange("p s t (h d) -> p (s t h) d", d=D)
        src = o.src[:, :, :, :].rearrange("p s t (h d) -> p s (t h) d", d=D)
        stat = lambda k: b.stat[:, :, :, :].rearrange("p t h (s k) -> p s (t h) k", k=S)[:, :, :, k]
        all_ = lambda a: a.rearrange("p s g d -> p (s g) d")

        @block.vector
        def _(ve):
            step = Steps(ve)
            loaded(m, ve, "l1b", "rows")
            mean = b.mean[:, :, :].rearrange("p s g -> p (s g)")
            step(ve.tensor_reduce(mean, groups_, X, ALU.add), s.mean)
            step(ve.tensor_scalar(b.mean[:, :, :], b.mean[:, :, :], 1.0 / D, None, ALU.mult), s.mean)
            step(ve.tensor_copy(stat(0), b.mean[:, :, :]), s.mean_kept)
            step(ve.tensor_tensor(all_(b.centred[:, :, :, :]), groups_,
                                  mean.unsqueeze(2).to_broadcast([P, S * G, D]), ALU.subtract), s.centred)
            step(ve.tensor_reduce(stat(2), src, X, ALU.add, apply_absolute_value=True), s.size)
            step(ve.tensor_scalar(stat(2), stat(2), 1.0 / D, None, ALU.mult), s.size)
            ve.wait_ge(s.squared, 1)
            step(ve.tensor_reduce(stat(3), b.square0[:, :, :, :], X, ALU.add), s.l2_in)
            ve.wait_ge(s.square2, 1)
            step(ve.tensor_reduce(stat(1), b.square[:, :, :, :], X, ALU.add), s.var)
            step(ve.tensor_scalar(stat(1), stat(1), 1.0 / D, None, ALU.mult), s.var)
            ve.wait_ge(s.down, 1)
            step(ve.tensor_tensor(b.logit[:, :, :], m.ps[:, 5, 0:G * S].rearrange("p (g s) -> p g s", s=S),
                                  w.mlp2_b.unsqueeze(1).to_broadcast([P, G, S]), ALU.add), s.logit)
            step(ve.tensor_scalar(b.logit[:, :, :], b.logit[:, :, :], m.cool[:, 0:1], None, ALU.mult), s.logit)
            step(ve.tensor_reduce(b.peak[:, :], b.logit[:, :, :], X, ALU.max), s.low)
            step(ve.tensor_tensor(b.logit[:, :, :], b.logit[:, :, :], b.peak[:, :].unsqueeze(2).to_broadcast([P, G, S]),
                                  ALU.subtract), s.low)
            ve.wait_ge(s.exps, 1)
            for r in range(2):
                step(ve.tensor_reduce(b.total[:, :], b.logit[:, :, :], X, ALU.add), s.floored)
                step(ve.reciprocal(b.total[:, :], b.total[:, :]), s.floored)
                step(ve.tensor_tensor(b.logit[:, :, :], b.logit[:, :, :],
                                      b.total[:, :].unsqueeze(2).to_broadcast([P, G, S]), ALU.mult), s.floored)
                if r == 0:
                    step(ve.tensor_scalar(b.logit[:, :, :], b.logit[:, :, :], 0.02, None, ALU.max), s.floored)
            step(ve.tensor_tensor(b.logit[:, :, 0].rearrange("p (t h) -> p t h", h=H),
                                  b.logit[:, :, 0].rearrange("p (t h) -> p t h", h=H),
                                  m.keep[:, :].unsqueeze(1).to_broadcast([P, NT, H]), ALU.add), s.floored)
            for k in range(S):
                step(ve.tensor_tensor(b.square[:, k, :, :], src[:, k, :, :],
                                      b.logit[:, :, k].unsqueeze(2).to_broadcast([P, G, D]), ALU.mult), s.product)
            step(ve.tensor_tensor(b.mixed[:, :, :], b.square[:, 0, :, :], b.square[:, 1, :, :], ALU.add), s.mix)
            step(ve.tensor_tensor(b.mixed[:, :, :], b.mixed[:, :, :], b.square[:, 2, :, :], ALU.add), s.mix)
            step(ve.tensor_tensor(b.mixed[:, :, :], b.mixed[:, :, :], b.square[:, 3, :, :], ALU.add), s.mix)
            ve.wait_ge(s.osq, 1)
            step(ve.tensor_reduce(b.sq[:, :], b.square[:, 0, :, :], X, ALU.add), s.orms)
            step(ve.tensor_scalar(b.sq[:, :], b.sq[:, :], 1.0 / D, 1e-5, ALU.mult, ALU.add), s.orms)
            ve.wait_ge(s.oroot, 1)
            step(ve.tensor_tensor(b.mixed[:, :, :], b.mixed[:, :, :], b.rms[:, :].unsqueeze(2).to_broadcast([P, G, D]),
                                  ALU.mult), s.normed)
            step(ve.tensor_tensor(b.mixed[:, :, :], b.mixed[:, :, :], w.norm_w.unsqueeze(1).to_broadcast([P, G, D]),
                                  ALU.mult), s.normed)
            ve.wait_ge(s.out, 1)
            step(ve.tensor_tensor(x[:, :, :], x[:, :, :], m.tiles(7), ALU.add), s.summed)

        @block.gpsimd
        def _(po):
            po.wait_ge(s.orms, 2)
            po.tensor_tensor(b.rms[:, :], b.sq[:, :], m.minus_half[:, 0:G], ALU.pow).then_inc(s.oroot, 1)

        @block.scalar
        def _(act):
            loaded(m, act, "l1b", "rows")
            act.activation(b.square0[:, :, :, :], src, ACT.Square).then_inc(s.squared, 1)
            act.wait_ge(s.centred, 1)
            act.activation(b.square[:, :, :, :], b.centred[:, :, :, :], ACT.Square).then_inc(s.square2, 1)
            act.wait_ge(s.l2_in, 1)
            act.activation(stat(3), stat(3), ACT.Sqrt).then_inc(s.l2, 1)
            act.wait_ge(s.turned, NT)
            act.activation(b.statT[:, :], m.ps[0:H * S * S, 4, :], ACT.Copy).then_inc(s.turned_copied, 1)
            for h in range(H):
                act.wait_ge(s.up, h + 1)
                act.activation(b.hidden[:, h, :], m.ps[:, h, :], ACT.Gelu_apprx_tanh, bias=w.mlp1_b
                               ).then_inc(s.hidden, 1)
            act.wait_ge(s.low, 2)
            act.activation(b.logit[:, :, :], b.logit[:, :, :], ACT.Exp).then_inc(s.exps, 1)
            act.wait_ge(s.mix, 3)
            act.activation(b.square[:, 0, :, :], b.mixed[:, :, :], ACT.Square).then_inc(s.osq, 1)
            act.wait_ge(s.oturned, NT)
            act.activation(b.oT[:, :], m.ps[:, 6, :], ACT.Copy).then_inc(s.ocopied, 1)

        @block.tensor
        def _(pe):
            loaded(m, pe, "l1b")
            for h in range(H):
                pe.matmul(m.ps[:, h, :], w.mlp1_x, xT[:, :], start=True, stop=False)
            pe.wait_ge(s.mean_kept, 1)
            pe.wait_ge(s.size, 2)
            pe.wait_ge(s.var, 2)
            pe.wait_ge(s.l2, 1)
            for t in range(NT):
                pe.transpose(m.ps[0:H * S * S, 4, tile_of(t)], b.stat[:, t, :, :].rearrange("p h k -> p (h k)"),
                             m.ident).then_inc(s.turned, 1)
            pe.wait_ge(s.turned_copied, 1)
            for h in range(H):
                pe.matmul(m.ps[:, h, :], w.mlp1_s[:, tile_of(h)], b.statT[:, :], start=False, stop=True
                          ).then_inc(s.up, 1)
            pe.wait_ge(s.hidden, H)
            for t in range(NT):
                for h in range(H):
                    at = (t * H + h) * S
                    mm = pe.matmul(m.ps[:, 5, at:at + S], tile(b.hidden[:, h, :], t), w.mlp2, start=True, stop=True)
            mm.then_inc(s.down, 1)
            pe.wait_ge(s.normed, 2)
            for t in range(NT):
                pe.transpose(m.tiles(6)[:, t, :], b.mixed[:, H * t:H * t + H, :].rearrange("p h d -> p (h d)"),
                             m.ident).then_inc(s.oturned, 1)
            pe.wait_ge(s.ocopied, 1)
            for t in range(NT):
                mm = pe.matmul(m.tiles(7)[:, t, :], tile(b.oT, t), w.d_wo, start=True, stop=True)
            mm.then_inc(s.out, 1)



def prepare(m, ctx):
    nc, w = m.nc, m.w
    CT, N, S = 2, 16, 16
    m.filter = ctx.enter_context(nc.sbuf_tensor("filter", [P, CT, T], F32))
    m.wide = ctx.enter_context(nc.sbuf_tensor("wide", [P, P], F32))
    m.w16 = ctx.enter_context(nc.sbuf_tensor("w16", [P, 3 * P], F16))
    m.cool = ctx.enter_context(nc.sbuf_tensor("cool", [P, 1], F32))
    m.keep = ctx.enter_context(nc.sbuf_tensor("keep", [P, 4], F32))
    with buffers(m, power=[P, 2, CT, N, N], ahead=[P, CT, S, N], back=[P, CT, S, N], product=[P, S, N, N], terms=[P, CT, N, N],
                 low=[P, 2, P]) as b, \
            stage(m, "step ahead low low_kept wide w16 keep temp_log cool") as (block, s):
        @block.vector
        def _(ve):
            step = Steps(ve)
            loaded(m, ve, "l2a")
            A = w.s_A.rearrange("p (c n k) -> p c n k", c=CT, n=N)
            flat_ = lambda a: a.rearrange("p s n k -> p (s n k)")
            src = A
            for i in range(4):
                for c in range(CT):
                    left = src[:, c, :, :].unsqueeze(2).to_broadcast([P, N, N, N])
                    right = src[:, c, :, :].rearrange("p k j -> p j k").unsqueeze(1).to_broadcast([P, N, N, N])
                    step(ve.tensor_tensor(b.product[:, :, :, :], left, right, ALU.mult), s.step)
                    step(ve.tensor_reduce(b.power[:, i % 2, c, :, :], b.product[:, :, :, :], X, ALU.add), s.step)
                src = b.power[:, i % 2, :, :, :]
            step(ve.tensor_copy(b.back[:, :, 0, :], w.s_C.rearrange("p (c n) -> p c n", c=CT)), s.step)
            for i in range(1, S):
                step(ve.tensor_tensor(b.product[:, 0:CT, :, :], src.rearrange("p c n k -> p c k n"),
                                      b.back[:, :, i - 1, :].unsqueeze(2).to_broadcast([P, CT, N, N]), ALU.mult), s.step)
                step(ve.tensor_reduce(b.back[:, :, i, :], b.product[:, 0:CT, :, :], X, ALU.add), s.step)
            ve.wait_ge(s.ahead, 1 + 5 * (S - 1))
            for c in range(CT):
                step(ve.tensor_tensor(b.product[:, :, :, :], b.back[:, c, :, :].unsqueeze(2).to_broadcast([P, S, S, N]),
                                      b.ahead[:, c, :, :].unsqueeze(1).to_broadcast([P, S, S, N]), ALU.mult), s.step)
                step(ve.tensor_reduce(m.filter[:, c, :].rearrange("p (j s) -> p j s", j=S), b.product[:, :, :, :], X,
                                      ALU.add), s.step)
            ve.wait_ge(s.low, 3)
            step(ve.tensor_tensor(m.wide[:, :], w.f_wide, m.ps[:, 2, 0:P], ALU.add), s.wide)
            loaded(m, ve, "l2b")
            step(ve.tensor_copy(m.w16[:, :], w.a_wqkv), s.w16)
            loaded(m, ve, "rows")
            ve.wait_ge(s.temp_log, 3)
            step(ve.scalar_tensor_tensor(m.cool[:, :], w.logit_temp, 0.0, m.cool[:, :], ALU.max, ALU.add), s.cool)
            step(ve.reciprocal(m.cool[:, :], m.cool[:, :]), s.cool)

        @block.gpsimd
        def _(po):
            step = Steps(po)
            loaded(m, po, "l2a")
            A = w.s_A.rearrange("p (c n k) -> p c n k", c=CT, n=N)
            step(po.tensor_copy(b.ahead[:, :, 0, :], w.s_B.rearrange("p (c n) -> p c n", c=CT)), s.ahead)
            for i in range(1, S):
                step(po.tensor_tensor(b.terms[:, :, :, :], A,
                                      b.ahead[:, :, i - 1, :].unsqueeze(2).to_broadcast([P, CT, N, N]), ALU.mult), s.ahead)
                for half in (8, 4, 2, 1):
                    out = b.terms[:, :, :, 0:half] if half > 1 else b.ahead[:, :, i, :].unsqueeze(3)
                    step(po.tensor_tensor(out, b.terms[:, :, :, 0:half], b.terms[:, :, :, half:2 * half], ALU.add),
                         s.ahead)

        @block.tensor
        def _(pe):
            loaded(m, pe, "l2f")
            RANK, DD, UD = 4, 100, 50
            pe.matmul(m.ps[0:RANK, 0, 0:P], w.f_down[0:DD, :], w.f_down_aux[0:DD, :], start=True, stop=True
                      ).then_inc(s.low, 1)
            pe.wait_ge(s.low_kept, 1)
            pe.matmul(m.ps[0:UD, 1, 0:P], w.f_up[0:RANK, :], b.low[0:RANK, 0, :], start=True, stop=True
                      ).then_inc(s.low, 1)
            pe.wait_ge(s.low_kept, 2)
            pe.matmul(m.ps[:, 2, 0:P], b.low[0:UD, 1, :], w.f_up_aux[0:UD, :], start=True, stop=True
                      ).then_inc(s.low, 1)

        @block.scalar
        def _(act):
            step = Steps(act)
            loaded(m, act, "rows")
            act.activation(m.keep[:, :], w.conv_res, ACT.Sigmoid).then_inc(s.keep, 1)
            step(act.activation(m.cool[:, :], w.logit_temp, ACT.Abs), s.temp_log)
            step(act.activation(m.cool[:, :], m.cool[:, :], ACT.Exp, scale=-1.0), s.temp_log)
            step(act.activation(m.cool[:, :], m.cool[:, :], ACT.Ln, bias=1.0), s.temp_log)
            act.wait_ge(s.low, 1)
            act.activation(b.low[0:4, 0, :], m.ps[0:4, 0, 0:P], ACT.Copy).then_inc(s.low_kept, 1)
            act.wait_ge(s.low, 2)
            act.activation(b.low[0:50, 1, :], m.ps[0:50, 1, 0:P], ACT.Copy).then_inc(s.low_kept, 1)



def state_space(m, x, tok, xT):
    w = m.w
    CT = 2
    BY_PE, BY_VECTOR = 54, 156
    RING = 6
    normalize(m, x, tok, flat(xT))
    with buffers(m, u=[P, CT, TOK], gate=[P, CT, TOK], y=[P, CT, TOK], late=[P, CT, TOK],
                 scaled=[P, RING, P],
                 product=[P, RING, SEQS, T]) as b, \
            stage(m, "projected kept gated scaled filtered tap product late y out biased summed") as (block, s):
        seqs = lambda a: a.rearrange("p (b t) -> p b t", b=SEQS)

        def filter_taps(eng, done, into, first, last):
            for i in range(first, last):
                for c in range(CT):
                    k = m.filter[:, c, i:i + 1]
                    u, y = seqs(b.u[:, c, :])[:, :, 0:T - i], seqs(into[:, c, :])[:, :, i:]
                    if i == first:
                        eng.tensor_scalar(y, u, k, None, ALU.mult).then_inc(done, 1)
                    else:
                        eng.wait_ge(done, CT * (i - first - 1) + c + 1)
                        eng.scalar_tensor_tensor(y, u, k, y, ALU.mult, ALU.add).then_inc(done, 1)

        @block.gpsimd
        def _(po):
            po.wait_ge(s.kept, CT)
            for i in range(BY_VECTOR, T):
                for c in range(CT):
                    n = CT * (i - BY_VECTOR) + c
                    y, add = seqs(b.late[:, c, :])[:, :, i:], b.product[:, n % RING, :, 0:T - i]
                    po.wait_ge(s.product, n + 1)
                    if i == BY_VECTOR:
                        po.tensor_copy(y, add).then_inc(s.late, 1)
                    else:
                        po.wait_ge(s.late, n + 1 - CT)
                        po.tensor_tensor(y, y, add, ALU.add).then_inc(s.late, 1)

        @block.tensor
        def _(pe):
            loaded(m, pe, "l2a")
            for c in range(2 * CT):
                pe.matmul(m.ps[:, c, :], tile(w.s_in, c), xT[:, :], start=True, stop=True).then_inc(s.projected, 1)
            pe.wait_ge(s.kept, CT)
            for i in range(BY_PE):
                for c in range(CT):
                    n = CT * i + c
                    pe.wait_ge(s.scaled, n + 1)
                    pe.matmul(seqs(m.ps[:, 5 + c, :])[:, :, i:], b.scaled[:, n % RING, :],
                              seqs(b.u[:, c, :])[:, :, 0:T - i], start=(i == 0), stop=(i == BY_PE - 1)
                              ).then_inc(s.filtered, 1)
            pe.wait_ge(s.y, 3 * CT)
            for t in range(NT):
                for c in range(CT):
                    mm = pe.matmul(m.tiles(4)[:, t, :], tile(b.y[:, c, :], t), tile(w.s_out, c), start=(c == 0),
                                   stop=(c == CT - 1))
            mm.then_inc(s.out, 1)

        @block.scalar
        def _(act):
            loaded(m, act, "l2a")
            for c in range(CT):
                act.wait_ge(s.projected, c + 1)
                act.activation(b.u[:, c, :], m.ps[:, c, :], ACT.Identity, bias=w.s_bias[:, c:c + 1]
                               ).then_inc(s.kept, 1)
            for c in range(CT):
                act.wait_ge(s.projected, CT + c + 1)
                act.activation(b.gate[:, c, :], m.ps[:, CT + c, :], ACT.Sigmoid,
                               bias=w.s_bias[:, CT + c:CT + c + 1]).then_inc(s.gated, 1)
            loaded(m, act, "const")

            def scale_diagonal(n):
                i, c = n // CT, n % CT
                if n >= RING:
                    act.wait_ge(s.filtered, n - RING + 1)
                act.activation(b.scaled[:, n % RING, :], m.ident, ACT.Copy, scale=m.filter[:, c, i:i + 1]
                               ).then_inc(s.scaled, 1)

            def product(n):
                i, c = BY_VECTOR + n // CT, n % CT
                if n >= RING:
                    act.wait_ge(s.late, n - RING + 1)
                act.activation(b.product[:, n % RING, :, 0:T - i], seqs(b.u[:, c, :])[:, :, 0:T - i], ACT.Copy,
                               scale=m.filter[:, c, i:i + 1]).then_inc(s.product, 1)

            act.wait_ge(s.kept, CT)
            DIAGONALS, PRODUCTS = CT * BY_PE, CT * (T - BY_VECTOR)
            done = 0
            for n in range(DIAGONALS):
                scale_diagonal(n)
                until = PRODUCTS * (n + 1) // DIAGONALS
                for k in range(done, until):
                    product(k)
                done = until

        @block.vector
        def _(ve):
            step = Steps(ve)
            loaded(m, ve, "rows")
            step(ve.tensor_tensor(x[:, :, :], x[:, :, :], m.rows("s_bout", NT), ALU.add), s.biased)
            ve.wait_ge(s.kept, CT)
            for c in range(CT):
                step(ve.memset(seqs(b.y[:, c, :])[:, :, 0:BY_PE], 0.0), s.biased)
            filter_taps(ve, s.tap, b.y, BY_PE, BY_VECTOR)
            ve.wait_ge(s.tap, CT * (BY_VECTOR - BY_PE))
            ve.wait_ge(s.gated, CT)
            for c in range(CT):
                y = seqs(b.y[:, c, :])
                ve.wait_ge(s.filtered, CT * BY_PE)
                step(ve.tensor_tensor(y, y, seqs(m.ps[:, 5 + c, :]), ALU.add), s.y)
                ve.wait_ge(s.late, CT * (T - BY_VECTOR))
                step(ve.tensor_tensor(y[:, :, BY_VECTOR:], y[:, :, BY_VECTOR:],
                                      seqs(b.late[:, c, :])[:, :, BY_VECTOR:], ALU.add), s.y)
                step(ve.tensor_tensor(b.y[:, c, :], b.y[:, c, :], b.gate[:, c, :], ALU.mult), s.y)
            ve.wait_ge(s.out, 1)
            step(ve.tensor_tensor(x[:, :, :], x[:, :, :], m.tiles(4), ALU.add), s.summed)



def low_rank_linear(m, x, tok, xT):
    w = m.w
    normalize(m, x, tok, flat(xT))
    with stage(m, "out biased summed") as (block, s):
        @block.tensor
        def _(pe):
            for t in range(NT):
                mm = pe.matmul(m.tiles(4)[:, t, :], tile(xT, t), m.wide[:, :], start=True, stop=True)
            mm.then_inc(s.out, 1)

        @block.vector
        def _(ve):
            step = Steps(ve)
            loaded(m, ve, "rows")
            step(ve.tensor_tensor(x[:, :, :], x[:, :, :], m.rows("f_b", NT), ALU.add), s.biased)
            ve.wait_ge(s.out, 1)
            step(ve.tensor_tensor(x[:, :, :], x[:, :, :], m.tiles(4), ALU.add), s.summed)



def mixed_attention(m, x, tok, xT):
    w = m.w
    LOW = 32
    HI = P - LOW
    normalize(m, x, tok, flat(xT))
    with buffers(m, x16=([P, TOK], F16), low=([P, 2, 3, TOK], F16), qk=[P, 2, TOK], v=[P, NT, P],
                 probs=[P, NT, T], peak=[P, NT], total=[P, NT], pT=[P, SEQS, TPS, T], yT=[P, TOK]) as b, \
            stage(m, "x16 made low part whole q_scaled scores peak exps inverse share turned turned_kept "
                     "y y_kept out biased summed") as (block, s):
        @block.tensor
        def _(pe):
            loaded(m, pe, "l2b")
            pe.wait_ge(s.x16, 1)

            def three(r, first, high, last, lhs, rhs, lhs16, rhs16):
                pe.matmul(first, lhs16[0:LOW], rhs16[0:LOW], start=True, stop=True, tile_position=(0, 0))
                pe.matmul(last, lhs16[HI:P], rhs16[HI:P], start=True, stop=True, tile_position=(HI, 0))
                return pe.matmul(high, lhs, rhs, start=True, stop=True)

            for r in range(3):
                if r == 2:
                    pe.wait_ge(s.whole, 1)
                base = 3 * (r % 2)
                if r < 2:
                    mm = three(r, m.ps[:, base, :], m.ps[:, base + 1, :], m.ps[:, base + 2, :],
                               tile(w.a_high, r), xT[:, :], tile(m.w16, r), b.x16[:, :])
                else:
                    for t in range(NT):
                        mm = three(r, m.tiles(base)[:, t, :], m.tiles(base + 1)[:, t, :], m.tiles(base + 2)[:, t, :],
                                   tile(xT, t), tile(w.a_high, r), tile(b.x16, t), tile(m.w16, r))
                mm.then_inc(s.made, 1)
            pe.wait_ge(s.whole, 3)
            pe.wait_ge(s.q_scaled, 1)
            for t in range(NT):
                r = slice(t // TPS * T, t // TPS * T + T)
                pe.matmul(m.ps[:, 4 + t // 2, (t % 2) * T:(t % 2 + 1) * T], tile(b.qk[:, 0, :], t), b.qk[:, 1, r],
                          start=True, stop=True).then_inc(s.scores, 1)
            for t in range(NT):
                pe.wait_ge(s.share, t + 1)
                if t >= 2:
                    pe.wait_ge(s.turned_kept, t - 1)
                for j in range(TPS):
                    mm = pe.transpose(m.ps[:, t % 2, j * P:j * P + P], b.probs[:, t, j * P:j * P + P], m.ident)
                mm.then_inc(s.turned, 1)
            for q in range(SEQS):
                pe.wait_ge(s.turned_kept, TPS * (q + 1))
                for j in range(TPS):
                    mm = pe.matmul(m.ps[:, 6, q * T:q * T + T], b.v[:, q * TPS + j, :], b.pT[:, q, j, :],
                                   start=(j == 0), stop=(j == TPS - 1))
                mm.then_inc(s.y, 1)
            pe.wait_ge(s.y_kept, 1)
            for t in range(NT):
                mm = pe.matmul(m.tiles(7)[:, t, :], tile(b.yT, t), w.a_out, start=True, stop=True)
            mm.then_inc(s.out, 1)

        @block.scalar
        def _(act):
            for r in range(3):
                act.wait_ge(s.made, r + 1)
                for k in range(2):
                    act.activation(b.low[:, k, r, :], m.ps[:, 3 * (r % 2) + 2 * k, :], ACT.Copy).then_inc(s.low, 1)
            for t in range(NT):
                act.wait_ge(s.peak, 2 * (t // 2) + 2)
                act.activation(b.probs[:, t, :], m.ps[:, 4 + t // 2, (t % 2) * T:(t % 2 + 1) * T], ACT.Exp,
                               bias=b.peak[:, t:t + 1], accum_out=b.total[:, t:t + 1]).then_inc(s.exps, 1)
            for t in range(NT):
                act.wait_ge(s.turned, t + 1)
                act.activation(b.pT[:, t // TPS, :, tile_of(t % TPS)],
                               m.ps[:, t % 2, 0:T].rearrange("p (j i) -> p j i", j=TPS), ACT.Copy
                               ).then_inc(s.turned_kept, 1)
            act.wait_ge(s.y, SEQS)
            act.activation(b.yT[:, :], m.ps[:, 6, :], ACT.Copy).then_inc(s.y_kept, 1)

        @block.vector
        def _(ve):
            step = Steps(ve)
            loaded(m, ve, "rows")
            step(ve.tensor_copy(b.x16[:, :], xT[:, :]), s.x16)
            step(ve.tensor_tensor(x[:, :, :], x[:, :, :], m.rows("a_bout", NT), ALU.add), s.biased)
            for r in range(3):
                out = b.qk[:, r, :] if r < 2 else b.v[:, :, :].rearrange("p t n -> p (t n)")
                ve.wait_ge(s.low, 2 * r + 2)
                step(ve.tensor_tensor(out, b.low[:, 0, r, :], m.ps[:, 3 * (r % 2) + 1, :], ALU.add), s.part)
                step(ve.tensor_tensor(out, out, b.low[:, 1, r, :], ALU.add), s.whole)
            step(ve.tensor_scalar(b.qk[:, 0, :], b.qk[:, 0, :], float(np.float32(P) ** -0.5), None, ALU.mult),
                 s.q_scaled)
            ve.wait_ge(s.scores, NT)
            for t in range(NT):
                ve.tensor_reduce(b.peak[:, t:t + 1], m.ps[:, 4 + t // 2, (t % 2) * T:(t % 2 + 1) * T], X, ALU.max,
                                 negate=True).then_inc(s.peak, 1)
            for t in range(NT):
                ve.wait_ge(s.exps, t + 1)
                step(ve.reciprocal(b.total[:, t:t + 1], b.total[:, t:t + 1]), s.inverse)
                ve.tensor_scalar(b.probs[:, t, :], b.probs[:, t, :], b.total[:, t:t + 1], None, ALU.mult
                                 ).then_inc(s.share, 1)
            ve.wait_ge(s.out, 1)
            step(ve.tensor_tensor(x[:, :, :], x[:, :, :], m.tiles(7), ALU.add), s.summed)



def causal_attention_a(m, x, tok, xT):
    small_heads(m, x, tok, xT, m.w.c_qkv, m.w.c_out, "l3a", m.w.c_bqkv, "c_bout", True)


def causal_attention_b(m, x, tok, xT):
    small_heads(m, x, tok, xT, m.w.e_qkv, m.w.e_out, "l3b", None, None, False)


LAG_TURN, LAG_MIX = 3, 5


def head_jobs(groups, per_group, units):
    jobs = [("turn_k", 0), ("turn_q", 0)]
    for u in range(units + LAG_MIX):
        g, i = u // per_group, u % per_group
        if u < units:
            jobs.append(("score", u))
        if g + 1 < groups and i == 0:
            jobs.append(("turn_k", g + 1))
        if g + 1 < groups and i == 2:
            jobs.append(("turn_q", g + 1))
        if LAG_TURN <= u < units + LAG_TURN:
            jobs.append(("turn", u - LAG_TURN))
        if u >= LAG_MIX:
            done, last = divmod(u - LAG_MIX, per_group)
            if last == 0 and done:
                jobs.append(("turn_out", done - 1))
            jobs.append(("mix", u - LAG_MIX))
            if last == per_group - 1:
                jobs.append(("keep", done))
    return jobs + [("turn_out", groups - 1)]


def small_heads(m, x, tok, xT, w_qkv, w_out, group, bias, out_bias, rotary):
    H, D, W = 16, 8, 32
    HG = P // W
    GROUPS = H // HG
    BANK = 512
    PER_SEQ = 3
    PER = SEQS * PER_SEQ
    UNITS = GROUPS * PER
    RING, RING_T = 4, 3
    JOBS = head_jobs(GROUPS, PER, UNITS)
    turns = [j for j in JOBS if j[0] in ("turn_k", "turn_q", "turn_out")]

    def unit(u):
        g, q, part = u // PER, u % PER // PER_SEQ, u % PER_SEQ
        return g, q, (range(HG) if part == 0 else range(2 * part - 2, 2 * part)), part == 0

    def exps_of(u):
        return sum(len(unit(k)[2]) for k in range(u + 1))

    normalize(m, x, tok, flat(xT))
    with buffers(m, qkv=[P, NT, 3 * P], wide=[P, 3, NT, H, W], qT=[P, 2, TOK], k_apart=[P, 2, HG, TOK],
                 peak=[P, RING, HG], probs=[P, RING, BANK], turned=[P, RING_T, HG, P], outT=[P, TOK],
                 inverse=[P, NT * HG], o=[P, NT, P]) as b, \
            stage(m, "projected kept blank placed rotated v turned_in q_kept k_apart scores peak exps turned "
                     "turned_kept mixed mixed_kept inverse normed oturned okept out biased summed") as (block, s):
        @block.tensor
        def _(pe):
            loaded(m, pe, group, "const")
            for t in range(NT):
                pe.matmul(m.ps[:, t, 0:3 * P], tile(xT, t), w_qkv, start=True, stop=True).then_inc(s.projected, 1)

            def turn_in(job):
                kind, g = job
                n = turns.index(job)
                if n >= 1:
                    last, lg = turns[n - 1]
                    pe.wait_ge({"turn_k": s.k_apart, "turn_q": s.q_kept, "turn_out": s.normed}[last], lg + 1)
                if kind == "turn_out":
                    pe.wait_ge(s.mixed_kept, g + 1)
                for t in range(NT):
                    src = tile(b.outT, t) if kind == "turn_out" else b.wide[
                        :, 1 if kind == "turn_k" else 0, t, HG * g:HG * g + HG, :].rearrange("p h d -> p (h d)")
                    mm = pe.transpose(m.tiles(7)[:, t, :], src, m.ident)
                mm.then_inc(s.turned_in, 1)

            def score(u):
                g, q, heads, first = unit(u)
                if u >= RING:
                    pe.wait_ge(s.exps, exps_of(u - RING))
                pe.wait_ge(s.q_kept, g + 1)
                pe.wait_ge(s.k_apart, g + 1)
                at = q * T
                keys = P if first else T
                queries = slice(at, at + P) if first else slice(at + P, at + T)
                out = m.ps[:, u % RING, :].rearrange("p (h n) -> p h n", n=keys)
                pe.matmul(out, b.qT[:, g % 2, queries], b.k_apart[:, g % 2, heads[0]:heads[-1] + 1, at:at + keys],
                          start=True, stop=False, skip_group_check=True)
                pe.matmul(out[:, :, keys - P:keys], m.ident16[:, :],
                          m.after[:, :].unsqueeze(1).to_broadcast([P, len(heads), P]), start=False, stop=True,
                          skip_group_check=True).then_inc(s.scores, 1)

            def turn(u):
                pe.wait_ge(s.exps, exps_of(u))
                if u >= 2:
                    pe.wait_ge(s.turned_kept, u - 1)
                for k in range(HG):
                    mm = pe.transpose(m.tiles(4 + u % 2)[:, k, :], tile(b.probs[:, u % RING, :], k), m.ident)
                mm.then_inc(s.turned, 1)

            def mix(u):
                g, q, heads, first = unit(u)
                pe.wait_ge(s.turned_kept, u + 1)
                pe.wait_ge(s.v, 1)
                if u % PER == 0 and g >= 1:
                    pe.wait_ge(s.mixed_kept, g)
                at = q * T + (0 if first else P)
                tiles = 1 if first else TPS
                for n, j in enumerate(heads):
                    for i in range(tiles):
                        mm = pe.matmul(m.ps[W * j:W * j + W, 6, at:at + P], b.wide[:, 2, TPS * q + i, HG * g + j, :],
                                       b.turned[:, u % RING_T, tiles * n + i, :], start=(i == 0), stop=(i == tiles - 1),
                                       tile_position=(0, W * j), skip_group_check=True)
                mm.then_inc(s.mixed, 1)

            pe.wait_ge(s.placed, 1)
            pe.wait_ge(s.kept, NT)
            for job in JOBS:
                if job[0] == "score":
                    score(job[1])
                elif job[0] == "turn":
                    turn(job[1])
                elif job[0] == "mix":
                    mix(job[1])
                elif job in turns:
                    turn_in(job)
            pe.wait_ge(s.normed, GROUPS)
            for t in range(NT):
                mm = pe.transpose(m.tiles(0)[:, t, :], b.o[:, t, :], m.ident)
            mm.then_inc(s.oturned, 1)
            pe.wait_ge(s.okept, 1)
            for t in range(NT):
                mm = pe.matmul(m.tiles(1)[:, t, :], tile(b.outT, t), w_out, start=True, stop=True)
            mm.then_inc(s.out, 1)

        @block.scalar
        def _(act):
            for t in range(NT):
                act.wait_ge(s.projected, t + 1)
                act.activation(b.qkv[:, t, :], m.ps[:, t, 0:3 * P], ACT.Copy).then_inc(s.kept, 1)
            for job in JOBS:
                kind, n = job
                if kind == "turn_q":
                    act.wait_ge(s.turned_in, turns.index(job) + 1)
                    act.activation(b.qT[:, n % 2, :], m.ps[:, 7, :], ACT.Copy).then_inc(s.q_kept, 1)
                elif kind == "score":
                    act.wait_ge(s.peak, n + 1)
                    if n >= RING:
                        act.wait_ge(s.turned, n - RING + 1)
                    heads, first = unit(n)[2:]
                    keys = P if first else T
                    for k in range(len(heads)):
                        act.activation(b.probs[:, n % RING, k * keys:(k + 1) * keys],
                                       m.ps[:, n % RING, k * keys:(k + 1) * keys], ACT.Exp,
                                       bias=b.peak[:, n % RING, k:k + 1]).then_inc(s.exps, 1)
                elif kind == "keep":
                    act.wait_ge(s.mixed, PER * (n + 1))
                    act.activation(b.outT[:, :], m.ps[:, 6, :], ACT.Copy).then_inc(s.mixed_kept, 1)
            act.wait_ge(s.oturned, 1)
            act.activation(b.outT[:, :], m.ps[:, 0, :], ACT.Copy).then_inc(s.okept, 1)

        @block.gpsimd
        def _(po):
            po.memset(b.wide[:, :, :, :, D:], 0.0).then_inc(s.blank, 1)
            po.wait_ge(s.blank, 1)
            po.memset(b.wide[:, 2, :, :, D:D + 1], 1.0).then_inc(s.blank, 1)
            if bias is None:
                po.wait_ge(s.kept, NT)
            else:
                po.wait_ge(s.rotated, 1)
            po.tensor_copy(b.wide[:, 2, :, :, 0:D], b.qkv[:, :, 2 * P:3 * P].rearrange("p t (h d) -> p t h d", d=D)
                           ).then_inc(s.v, 1)

        @block.vector
        def _(ve):
            step = Steps(ve)
            ve.wait_ge(s.kept, NT)
            if bias is not None:
                loaded(m, ve, "rows")
                step(ve.tensor_tensor(b.qkv[:, :, :], b.qkv[:, :, :], bias.unsqueeze(1).to_broadcast([P, NT, 3 * P]),
                                      ALU.add), s.rotated)
            heads = b.qkv[:, :, :].rearrange("p t (h d) -> p t h d", d=D)
            if rotary:
                loaded(m, ve, "const")
                F = D // 2
                part = b.k_apart[:, 0, :, :].rearrange("p k (t h f) -> p k t h f", t=NT, f=F)
                pairs = b.qkv[:, :, 0:2 * P].rearrange("p t (h f e) -> p t h f e", f=F, e=2)
                table = lambda k: m.w.rope[:, k * NT * F:(k + 1) * NT * F].rearrange(
                    "p (t f) -> p t f", t=NT).unsqueeze(2).to_broadcast([P, NT, 2 * H, F])
                for k, (e, tab) in enumerate(((0, 0), (1, 1), (0, 1), (1, 0))):
                    step.tell(ve.tensor_tensor(part[:, k, :, :, :], pairs[:, :, :, :, e], table(tab), ALU.mult),
                              s.rotated)
                ve.wait_ge(s.rotated, step.count(s.rotated))
                for r in range(2):
                    hs = slice(H * r, H * r + H)
                    step.tell(ve.tensor_tensor(b.wide[:, r, :, :, 0:F], part[:, 0, :, hs, :], part[:, 1, :, hs, :],
                                               ALU.subtract), s.rotated)
                    step.tell(ve.tensor_tensor(b.wide[:, r, :, :, F:D], part[:, 2, :, hs, :], part[:, 3, :, hs, :],
                                               ALU.add), s.rotated)
            else:
                for r in range(2):
                    step.tell(ve.tensor_copy(b.wide[:, r, :, :, 0:D], heads[:, :, H * r:H * r + H, :]), s.rotated)
            ve.wait_ge(s.rotated, step.count(s.rotated))
            ve.wait_ge(s.blank, 2)
            step(ve.memset(b.inverse[:, 0:1], 0.0), s.placed)
            if out_bias is not None:
                step(ve.tensor_tensor(x[:, :, :], x[:, :, :], m.rows(out_bias, NT), ALU.add), s.biased)
            loaded(m, ve, "const")
            for job in JOBS:
                kind, n = job
                if kind == "turn_k":
                    ve.wait_ge(s.turned_in, turns.index(job) + 1)
                    ve.scalar_tensor_tensor(b.k_apart[:, n % 2, :, :], m.ps[:, 7, :].unsqueeze(1).to_broadcast([P, HG, TOK]),
                                            float(D) ** -0.5,
                                            m.w.heads32[:, 0:P:W].unsqueeze(2).to_broadcast([P, HG, TOK]),
                                            ALU.mult, ALU.mult).then_inc(s.k_apart, 1)
                elif kind == "score":
                    ve.wait_ge(s.scores, n + 1)
                    heads, first = unit(n)[2:]
                    ve.tensor_reduce(b.peak[:, n % RING, 0:len(heads)],
                                     m.ps[:, n % RING, :].rearrange("p (h n) -> p h n", h=len(heads)), X, ALU.max,
                                     negate=True).then_inc(s.peak, 1)
                elif kind == "turn":
                    ve.wait_ge(s.turned, n + 1)
                    if n >= RING_T:
                        ve.wait_ge(s.mixed, n - RING_T + 1)
                    ve.tensor_copy(b.turned[:, n % RING_T, :, :], m.tiles(4 + n % 2)).then_inc(s.turned_kept, 1)
                elif kind == "turn_out":
                    ve.wait_ge(s.turned_in, turns.index(job) + 1)
                    out = m.ps[:, 7, :].rearrange("p (t h d) -> p t h d", t=NT, h=HG)
                    inv = b.inverse[:, :].rearrange("p (t h) -> p t h", t=NT)
                    step(ve.reciprocal(inv, out[:, :, :, D]), s.inverse)
                    step(ve.tensor_tensor(b.o[:, :, HG * D * n:HG * D * (n + 1)].rearrange("p t (h d) -> p t h d", d=D),
                                          out[:, :, :, 0:D], inv.unsqueeze(3).to_broadcast([P, NT, HG, D]), ALU.mult),
                         s.normed)
            ve.wait_ge(s.out, 1)
            step(ve.tensor_tensor(x[:, :, :], x[:, :, :], m.tiles(1), ALU.add), s.summed)



def deep_network(m, x, tok, xT):
    w = m.w
    C = 4
    normalize(m, x, tok, flat(xT))
    with buffers(m, silu=[P, C, TOK], a=[P, C, TOK], b=[P, C, TOK], c=[P, C, TOK], y=[P, NT, P]) as b, \
            stage(m, "one two silu first h1 second h2 third out y summed") as (block, s):
        @block.tensor
        def _(pe):
            loaded(m, pe, "l3f")
            for c in range(C):
                pe.matmul(m.ps[:, c, :], tile(w.g_1, c), xT[:, :], start=True, stop=True).then_inc(s.one, 1)
                pe.matmul(m.ps[:, C + c, :], tile(w.g_2, c), xT[:, :], start=True, stop=True).then_inc(s.two, 1)
            for k, (weights, src, ready, made) in enumerate(((w.g_h1, b.a, s.first, s.h1), (w.g_h2, b.b, s.second, s.h2))):
                for o in range(C):
                    bank = C * k + o
                    if k == 0:
                        pe.wait_ge(s.silu, o + 1)
                    else:
                        pe.wait_ge(s.first, o + 1)
                    for c in range(C):
                        if o == 0:
                            pe.wait_ge(ready, c + 1)
                        mm = pe.matmul(m.ps[:, bank, :], weights[:, (c * C + o) * P:(c * C + o + 1) * P], src[:, c, :],
                                       start=(c == 0), stop=(c == C - 1))
                    mm.then_inc(made, 1)
            pe.wait_ge(s.third, C)
            for t in range(NT):
                for c in range(C):
                    mm = pe.matmul(m.tiles(0)[:, t, :], tile(b.c[:, c, :], t), tile(w.g_3, c), start=(c == 0),
                                   stop=(c == C - 1))
            mm.then_inc(s.out, 1)

        @block.scalar
        def _(act):
            loaded(m, act, "l3f")
            for c in range(C):
                act.wait_ge(s.one, c + 1)
                act.activation(b.silu[:, c, :], m.ps[:, c, :], ACT.Silu, scale=w.g_scales[:, c:c + 1]
                               ).then_inc(s.silu, 1)
            for k, (src, made, done) in enumerate(((b.b, s.h1, s.second), (b.c, s.h2, s.third))):
                for c in range(C):
                    act.wait_ge(made, c + 1)
                    act.activation(src[:, c, :], m.ps[:, C * k + c, :], ACT.Gelu,
                                   scale=w.g_scales[:, C * (2 + k) + c:C * (2 + k) + c + 1]).then_inc(done, 1)

        @block.vector
        def _(ve):
            step = Steps(ve)
            loaded(m, ve, "l3f", "rows")
            for c in range(C):
                ve.wait_ge(s.two, c + 1)
                ve.wait_ge(s.silu, c + 1)
                ve.scalar_tensor_tensor(b.a[:, c, :], m.ps[:, C + c, :], w.g_scales[:, C + c:C + c + 1], b.silu[:, c, :],
                                        ALU.mult, ALU.mult).then_inc(s.first, 1)
            ve.wait_ge(s.out, 1)
            step(ve.tensor_tensor(b.y[:, :, :], m.tiles(0), m.rows("g_s3", NT), ALU.mult), s.y)
            step(ve.tensor_tensor(x[:, :, :], x[:, :, :], b.y[:, :, :], ALU.add), s.summed)



SUBLAYERS = (mamba, experts, linear_attention, experts, windowed_attention, channel_mix, delta_rule, channel_mix,
             state_space, low_rank_linear, mixed_attention, low_rank_linear, causal_attention_a, deep_network,
             causal_attention_b, deep_network)

class Machine:
    pass


def program(nc, a, out, spans):
    with ExitStack() as ctx:
        m = Machine()
        m.nc, m.stages, m.made, m.resting, m.load = nc, 0, 0, [], {}
        m.ps = ctx.enter_context(nc.psum_tensor("ps", [P, 8, 512], F32))
        m.tiles = lambda bank: m.ps[:, bank, :].rearrange("p (t n) -> p t n", t=NT)
        held = {}
        found = {}
        for group, parts in spans.items():
            held[group] = ctx.enter_context(nc.sbuf_tensor(f"held_{group}", [P, sum(c for _, _, c in parts)], F32))
            at = 0
            for name, rows, cols in parts:
                found[name] = held[group][0:rows, at:at + cols]
                at += cols
        m.w = Named(found)
        m.ident, m.heads8 = m.w.ident, m.w.heads8
        m.rows = lambda name, n: found[name].unsqueeze(1).to_broadcast([P, n, P])
        m.minus_half = ctx.enter_context(nc.sbuf_tensor("minus_half", [P, 64], F32))
        m.ident16 = ctx.enter_context(nc.sbuf_tensor("ident16", [P, P], BF16))
        m.after = ctx.enter_context(nc.sbuf_tensor("after16", [P, P], BF16))
        x = ctx.enter_context(nc.sbuf_tensor("x", [P, NT, P], F32))
        tok = ctx.enter_context(nc.sbuf_tensor("tok", [P, NT, P], F32))
        xT = ctx.enter_context(nc.sbuf_tensor("xT", [P, TOK], F32))
        for group in spans:
            m.load[group] = ctx.enter_context(nc.semaphore(f"load_{group}"))
        started = ctx.enter_context(nc.semaphore("started"))

        with nc.Block() as block:
            @block.sync
            def _(sp):
                for group, parts in spans.items():
                    src = a[group]
                    if group == "rows":
                        src = src.to_broadcast([P, src.shape[1]])
                    sp.dma_start(held[group][:, :], src).then_inc(m.load[group], 16)
                sp.wait_ge(m.load["const"], 16)

            @block.gpsimd
            def _(po):
                po.memset(m.minus_half[:, :], -0.5).then_inc(started, 1)
                loaded(m, po, "const")
                for out, src in ((m.ident16, m.ident), (m.after, m.w.after)):
                    po.tensor_copy(out[:, :], src).then_inc(started, 1)
                po.wait_ge(started, 3)

        prepare(m, ctx)
        with nc.Fori(0, PASSES) as i:
            with stage(m, "x_in") as (block, s):
                @block.sync
                def _(sp):
                    sp.dma_start(x[:, :, :], a["x"][bass.ds(i * SEQS, SEQS)].rearrange("b (h p) d -> p (b h) d", p=P)
                                 ).then_inc(s.x_in, 16)
                    sp.wait_ge(s.x_in, 16)
            for layer in SUBLAYERS:
                layer(m, x, tok, xT)
            with stage(m, "x_out") as (block, s):
                @block.sync
                def _(sp):
                    sp.dma_start(out[bass.ds(i * SEQS, SEQS)].rearrange("b (h p) d -> p (b h) d", p=P), x[:, :, :]
                                 ).then_inc(s.x_out, 16)
                    sp.wait_ge(s.x_out, 16)
            nc.all_engine_barrier()



def chunks(a):
    import numpy as _np
    k = a.shape[0] // 128
    return _np.ascontiguousarray(a.reshape(k, 128, a.shape[1]).transpose(1, 0, 2)).reshape(128, k * a.shape[1])


def hide(hidden):
    import numpy as _np
    return _np.where(hidden, -1e30, 0.0).astype(_np.float32)


def groups(v):
    import numpy as _np
    col = lambda a: chunks(a.reshape(-1, 1))
    g = {}
    eye = _np.eye(128, dtype=_np.float32)
    g["const"] = {"ident": eye,
                  "heads8": _np.kron(_np.eye(16, dtype=_np.float32), _np.ones((8, 8), _np.float32))}
    at = _np.arange(128)
    half_turn = _np.zeros((128, 128), _np.float32)
    for i in range(128):
        half_turn[i + 32 if i % 64 < 32 else i - 32, i] = -1.0 if i % 64 < 32 else 1.0
    rates = (1.0 / 10000.0 ** (_np.arange(0, 64, 2, dtype=_np.float32) / _np.float32(64))).astype(_np.float32)
    angle = (_np.arange(256, dtype=_np.float32)[None, :] * rates[at % 32][:, None]).astype(_np.float64)
    near = _np.arange(192)[None, :] - at[:, None]
    band = ((near >= 0) & (near < 64)).astype(_np.float32)
    g["const"].update({
        "half_turn": half_turn, "heads64": _np.kron(_np.eye(2, dtype=_np.float32), _np.ones((64, 64), _np.float32)),
        "cosine": _np.cos(angle).astype(_np.float32), "sine": _np.sin(angle).astype(_np.float32),
        "band": _np.concatenate([band, band[:, 0:128]], axis=1), "tiny": _np.full((128, 1), 1e-12, _np.float32)})
    chunk = at // 32
    same = chunk[:, None] == chunk[None, :]
    g["const"].update({
        "heads32": same.astype(_np.float32),
        "minus_low": -(same & (at[:, None] > at[None, :])).astype(_np.float32),
        "minus_high": -(same & (at[:, None] < at[None, :])).astype(_np.float32),
        "upto": (same & (at[:, None] <= at[None, :])).astype(_np.float32)})
    theta = (1.0 / 10000.0 ** (_np.arange(4, dtype=_np.float32) / _np.float32(4))).astype(_np.float32)
    times = (_np.arange(4)[None, :] % 2 * 128 + at[:, None]).astype(_np.float32)
    angle = (times[:, :, None] * theta[None, None, :]).astype(_np.float64).reshape(128, 16)
    g["const"].update({
        "rope": _np.concatenate([_np.cos(angle), _np.sin(angle)], axis=1).astype(_np.float32),
        "after": hide(at[None, :] > at[:, None])})
    n = "L0_attn_a_"
    g["l0a"] = {"in_proj": v[n + "in_proj_w"], "conv_w": chunks(v[n + "conv_w"][:, 0, :]),
                "conv_b": col(v[n + "conv_b"]), "x_proj": chunks(v[n + "x_proj_w"]),
                "dt_proj": v[n + "dt_proj_w"], "dt_bias": col(v[n + "dt_proj_b"]), "A_log": chunks(v[n + "A_log"]),
                "D": col(v[n + "D"]), "out_proj": chunks(v[n + "out_proj_w"])}
    n = "L0_ffn_"
    wi = _np.concatenate([v[n + "gate_wi"]] + [e for e in v[n + "exp_wi"]], axis=1)
    wo = _np.concatenate([v[n + "gate_wo"]] + [e for e in v[n + "exp_wo"]], axis=0)
    bi = _np.concatenate([v[n + "gate_bi"], v[n + "exp_bi"].reshape(-1)])
    g["ffn"] = {"ffn_wi": wi, "ffn_wo": chunks(wo), "ffn_bi": col(bi), "exp_bo": v[n + "exp_bo"]}
    n = "L0_attn_b_"
    g["l0b"] = {"ln_g": col(v[n + "ln_g"]), "ln_b": col(v[n + "ln_b"]), "l0_wq": v[n + "Wq"].T,
                "l0_wk": v[n + "Wk"].T, "l0_wv": v[n + "Wv"].T, "l0_bk": col(v[n + "bk"])}
    g["rows"] = {"gate_bo": v["L0_ffn_gate_bo"], "l0_bq": v[n + "bq"], "l0_bv": v[n + "bv"]}
    n = "L1_attn_a_"
    taps = _np.concatenate([v[n + "cqw"], v[n + "ckw"], v[n + "cvw"]], axis=0)
    g["l1a"] = {"l1_wqkv": _np.concatenate([v[n + "Wq"].T, v[n + "Wk"].T, v[n + "Wv"].T], axis=1),
                "l1_bqkv": col(_np.concatenate([v[n + "bq"], v[n + "bk"], v[n + "bv"]])), "l1_taps": chunks(taps),
                "l1_tap_bias": col(_np.concatenate([v[n + "cqb"], v[n + "ckb"], v[n + "cvb"]])),
                "l1_wo": chunks(v[n + "Wo"].T)}
    g["rows"]["l1_bo"] = v[n + "bo"]
    n = "L1_ffn_"
    g["l1f"] = {"l1_wr": v[n + "W_r"].T, "l1_wk": v[n + "W_k"].T, "l1_wv": v[n + "W_v"].T,
                "mu": _np.stack([v[n + "mu_k"], v[n + "mu_r"]], axis=1)}
    n = "L1_attn_b_"
    mlp1 = v[n + "mlp1_w"]
    stats = _np.zeros((64, 4, 128), _np.float32)
    for head in range(4):
        stats[16 * head:16 * head + 16, head, :] = mlp1[:, 128:].T
    g["l1b"] = {"d_wqkv": _np.concatenate([v[n + "q_w"].T, v[n + "k_w"].T, v[n + "v_w"].T], axis=1),
                "d_wb": v[n + "b_w"].T, "d_wo": v[n + "o_w"].T, "mlp1_x": mlp1[:, 0:128].T,
                "d_taps": _np.concatenate([v[n + "q_cw"], v[n + "k_cw"], v[n + "v_cw"]], axis=1),
                "d_short": v[n + "fir_short_w"].reshape(128, 5), "d_long": v[n + "fir_long_w"].reshape(128, 64),
                "mlp1_s": stats.reshape(64, 512), "mlp1_b": col(v[n + "mlp1_b"]), "mlp2": v[n + "mlp2_w"].T}
    g["rows"].update({"mlp2_b": v[n + "mlp2_b"], "logit_temp": v[n + "logit_temp"],
                      "conv_res": v[n + "conv_res_logit"], "norm_w": v[n + "norm_w"]})
    n = "L2_attn_a_"
    g["l2a"] = {"s_A": chunks(v[n + "A"].reshape(256, 256)), "s_B": chunks(v[n + "B_ssm"]),
                "s_C": chunks(v[n + "C_ssm"]), "s_in": _np.concatenate([v[n + "w_in"], v[n + "w_gate"]], axis=1),
                "s_bias": col(_np.concatenate([v[n + "b_in"], v[n + "b_gate"]])), "s_out": chunks(v[n + "w_out"])}
    g["rows"]["s_bout"] = v[n + "b_out"]
    n = "L2_ffn_"
    g["l2f"] = {"f_wide": v[n + "W"].T, "f_down": v[n + "lora_down"].T, "f_down_aux": v[n + "down_aux"],
                "f_up": v[n + "lora_up"].T, "f_up_aux": v[n + "up_aux"].T}
    g["rows"]["f_b"] = v[n + "b"]
    n = "L2_attn_b_"
    high = v[n + "weight_qkv"].copy()
    high[0:32] = 0.0
    high[96:128] = 0.0
    g["l2b"] = {"a_wqkv": v[n + "weight_qkv"], "a_high": high, "a_out": v[n + "out_w"].T}
    g["rows"]["a_bout"] = v[n + "out_b"]
    n = "L3_attn_a_"
    g["l3a"] = {"c_qkv": _np.concatenate([v[n + "W_q"].T, v[n + "W_k"].T, v[n + "W_v"].T], axis=1),
                "c_out": v[n + "W_o"].T}
    g["rows"].update({"c_bqkv": _np.concatenate([v[n + "b_q"], v[n + "b_k"], v[n + "b_v"]]), "c_bout": v[n + "b_o"]})
    n = "L3_attn_b_"
    g["l3b"] = {"e_qkv": v[n + "w_qkv"].T, "e_out": v[n + "w_out"].T}
    n = "L3_ffn_"
    g["l3f"] = {"g_1": v[n + "w1_w"].T, "g_2": v[n + "w2_w"].T, "g_h1": chunks(v[n + "h1_w"].T),
                "g_h2": chunks(v[n + "h2_w"].T), "g_3": chunks(v[n + "w3_w"].T),
                "g_scales": col(_np.concatenate([v[n + "w1_s"], v[n + "w2_s"], v[n + "h1_s"], v[n + "h2_s"]]))}
    g["rows"]["g_s3"] = v[n + "w3_s"]
    first = ("const", "l2a", "l2f", "l2b", "rows")
    return {name: g[name] for name in first + tuple(n for n in g if n not in first)}


def lay_out(v):
    import numpy as _np
    arrays, spans = {}, {}
    for name, parts in groups(v).items():
        spans[name], made = [], []
        for key, a in parts.items():
            if name == "rows":
                a = a.reshape(1, -1)
                spans[name].append((key, 128, a.shape[1]))
                made.append(a)
                continue
            spans[name].append((key, a.shape[0], a.shape[1]))
            made.append(a if a.shape[0] == 128 else _np.concatenate(
                [a, _np.zeros((128 - a.shape[0], a.shape[1]), a.dtype)], axis=0))
        arrays[name] = _np.ascontiguousarray(_np.concatenate(made, axis=1))
    return arrays, spans


def kernel(**inputs):
    import numpy as _np
    import concourse.bacc as _bacc
    from concourse import mybir as _mybir
    from concourse.bass_utils import run_bass_kernel_spmd as _run

    v = {k: _np.asarray(a) for k, a in inputs.items()}
    arrays, spans = lay_out(v)
    arrays["x"] = _np.ascontiguousarray(v["L0_attn_a_x"])
    nc = _bacc.Bacc("TRN2", target_bir_lowering=False, num_devices=1)
    args = {}
    for name, a in arrays.items():
        args[name] = nc.dram_tensor(f"in_{name}", a.shape, _mybir.dt.from_np(a.dtype), kind="ExternalInput").ap()
    out = nc.dram_tensor("out_0", v["L0_attn_a_x"].shape, _mybir.dt.float32, kind="ExternalOutput").ap()
    program(nc, args, out, spans)
    r = _run(nc, [{f"in_{name}": a for name, a in arrays.items()}], core_ids=[0])
    return r.results[0]["out_0"]
```
